# Optimizing a Trainium2 kernel written in Bass

```python
import numpy as np
import jax
import jax.numpy as jnp

def _softmax(x, axis=-1):
    return jax.nn.softmax(x, axis=axis)

def _gelu(x):
    return jax.nn.gelu(x, approximate=True)

def _silu(x):
    return jax.nn.silu(x)

def _sigmoid(x):
    return jax.nn.sigmoid(x)

def _layernorm(x, axis=-1, eps=1e-05):
    m = jnp.mean(x, axis=axis, keepdims=True)
    v = jnp.var(x, axis=axis, keepdims=True)
    return (x - m) / jnp.sqrt(v + eps)

def _scatter_add(tgt, idx, src, axis=0):
    return tgt.at[idx].add(src)

def _segment_sum(src, seg, n):
    return jax.ops.segment_sum(src, seg, n)
kernel_name = 'mk_perceiver_d1_seqx_r2_b9a3ae'

def setup_inputs(seed: int=0):
    np.random.seed(seed)
    _w = jnp.asarray

    def _rec_inputs():
        import jax
        import jax.numpy as jnp
        _rk = jax.random.key(seed)
        x = -0.0002928 + 1 * jax.random.normal(jax.random.fold_in(_rk, 1), (2, 512, 512), jnp.float32)
        _lenS = 512 - jax.random.randint(jax.random.fold_in(_rk, 7), (2,), 0, max(1, 512 // 4) + 1, jnp.int32)
        _lenS2 = 8192 - jax.random.randint(jax.random.fold_in(_rk, 8), (2,), 0, max(1, 8192 // 4) + 1, jnp.int32)
        _ctx_1024P = jax.random.normal(jax.random.fold_in(_rk, 11), (2, 16, 512), jnp.float32)
        _ctx_1024c = jax.random.dirichlet(jax.random.fold_in(_rk, 511), 0.3 * jnp.ones((16,), jnp.float32), (2, 8192))
        _ctx_1024t = jnp.einsum('bsk,bkd->bsd', _ctx_1024c, _ctx_1024P)
        _ctx_1024t = _ctx_1024t * jax.lax.rsqrt(jnp.mean(jnp.square(_ctx_1024t)) + 1e-12) * 0.953939
        ctx_1024 = -1.39393e-06 + 0.999914 * (_ctx_1024t + 0.3 * jax.random.normal(jax.random.fold_in(_rk, 611), (2, 8192, 512), jnp.float32))
        _validS = jnp.arange(512)[None, :] < _lenS[:, None]
        _validS2 = jnp.arange(8192)[None, :] < _lenS2[:, None]
        _causal = jnp.tril(jnp.ones((512, 512), dtype=bool))
        mask_BxS2_bf1 = jnp.ones((2, 8192), dtype=bool)
        return (x, ctx_1024, mask_BxS2_bf1)
    x, ctx_1024, mask_BxS2_bf1 = _rec_inputs()

    def _L0_xattn_setup():
        import jax, jax.numpy as jnp
        import numpy as np
        N_HEADS = 16
        D_MODEL = 512
        HEAD_DIM = D_MODEL // N_HEADS
        MASK_FILL = -100000000.0

        def _split_heads(x):
            B, S, _ = x.shape
            return x.reshape(B, S, N_HEADS, HEAD_DIM).transpose(0, 2, 1, 3)
        key = jax.random.key(seed)
        ks = jax.random.split(key, 12)
        B, L, P = (2, 1024, 1024)
        s = 1.0 / np.sqrt(D_MODEL).astype(np.float32)
        inp = {'q': jax.random.normal(ks[0], (B, L, D_MODEL), dtype=jnp.float32), 'k': jax.random.normal(ks[1], (B, P, D_MODEL), dtype=jnp.float32), 'v': jax.random.normal(ks[2], (B, P, D_MODEL), dtype=jnp.float32), 'attention_mask': jnp.ones((B, P), dtype=bool), 'Wq': jax.random.normal(ks[3], (D_MODEL, D_MODEL), dtype=jnp.float32) * s, 'bq': jnp.zeros((D_MODEL,), dtype=jnp.float32), 'Wk': jax.random.normal(ks[4], (D_MODEL, D_MODEL), dtype=jnp.float32) * s, 'bk': jnp.zeros((D_MODEL,), dtype=jnp.float32), 'Wv': jax.random.normal(ks[5], (D_MODEL, D_MODEL), dtype=jnp.float32) * s, 'bv': jnp.zeros((D_MODEL,), dtype=jnp.float32), 'Wo': jax.random.normal(ks[6], (D_MODEL, D_MODEL), dtype=jnp.float32) * s, 'bo': jnp.zeros((D_MODEL,), dtype=jnp.float32)}
        return inp
    _L0_xattn_all = _L0_xattn_setup()
    _L0_xattn_in = {k: v for k, v in _L0_xattn_all.items() if k in ('Wq', 'bq', 'Wk', 'bk', 'Wv', 'bv', 'Wo', 'bo')}
    del _L0_xattn_all

    def _L0_attn_setup():
        import jax, jax.numpy as jnp
        import numpy as np
        B, S, D = (2, 1024, 512)
        H, DH = (16, 64)
        SCALE = DH ** (-0.5)
        key = jax.random.key(seed)
        ks = jax.random.split(key, 5)

        def w(k, shape):
            return jax.random.normal(k, shape, dtype=jnp.float32) * 0.02
        return {'x': jax.random.normal(ks[0], (B, S, D), dtype=jnp.float32), 'Wq': w(ks[1], (D, H * DH)), 'Wk': w(ks[2], (D, H * DH)), 'Wv': w(ks[3], (D, H * DH)), 'Wo': w(ks[4], (H * DH, D)), 'bo': jnp.zeros((D,), dtype=jnp.float32)}
    _L0_attn_all = _L0_attn_setup()
    _L0_attn_in = {k: v for k, v in _L0_attn_all.items() if k in ('Wq', 'Wk', 'Wv', 'Wo', 'bo')}
    del _L0_attn_all

    def _L0_ffn_setup():
        import jax, jax.numpy as jnp
        import numpy as np
        CAPACITY = 2
        B, S, D, E, I = (4, 2048, 512, 8, 2048)
        key = jax.random.key(seed)
        k0, k1, k2, k3, k4 = jax.random.split(key, 5)
        x = jax.random.normal(k0, (B, S, D), dtype=jnp.float32)
        gate_w = jax.random.normal(k1, (E, D), dtype=jnp.float32) * 0.006
        w_gate = jax.random.normal(k2, (E, I, D), dtype=jnp.float32) * (1.0 / np.sqrt(D))
        w_up = jax.random.normal(k3, (E, I, D), dtype=jnp.float32) * (1.0 / np.sqrt(D))
        w_down = jax.random.normal(k4, (E, D, I), dtype=jnp.float32) * (1.0 / np.sqrt(I))
        return {'x': x, 'gate_w': gate_w, 'w_gate': w_gate, 'w_up': w_up, 'w_down': w_down}
    _L0_ffn_all = _L0_ffn_setup()
    _L0_ffn_in = {k: v for k, v in _L0_ffn_all.items() if k in ('gate_w', 'w_gate', 'w_up', 'w_down')}
    del _L0_ffn_all
    return {'x': x, 'ctx_1024': ctx_1024, 'mask_BxS2_bf1': mask_BxS2_bf1, 'L0_xattn_Wq': _L0_xattn_in['Wq'], 'L0_xattn_bq': _L0_xattn_in['bq'], 'L0_xattn_Wk': _L0_xattn_in['Wk'], 'L0_xattn_bk': _L0_xattn_in['bk'], 'L0_xattn_Wv': _L0_xattn_in['Wv'], 'L0_xattn_bv': _L0_xattn_in['bv'], 'L0_xattn_Wo': _L0_xattn_in['Wo'], 'L0_xattn_bo': _L0_xattn_in['bo'], 'L0_attn_Wq': _L0_attn_in['Wq'], 'L0_attn_Wk': _L0_attn_in['Wk'], 'L0_attn_Wv': _L0_attn_in['Wv'], 'L0_attn_Wo': _L0_attn_in['Wo'], 'L0_attn_bo': _L0_attn_in['bo'], 'L0_ffn_gate_w': _L0_ffn_in['gate_w'], 'L0_ffn_w_gate': _L0_ffn_in['w_gate'], 'L0_ffn_w_up': _L0_ffn_in['w_up'], 'L0_ffn_w_down': _L0_ffn_in['w_down']}

def reference(x, ctx_1024, mask_BxS2_bf1, L0_xattn_Wq, L0_xattn_bq, L0_xattn_Wk, L0_xattn_bk, L0_xattn_Wv, L0_xattn_bv, L0_xattn_Wo, L0_xattn_bo, L0_attn_Wq, L0_attn_Wk, L0_attn_Wv, L0_attn_Wo, L0_attn_bo, L0_ffn_gate_w, L0_ffn_w_gate, L0_ffn_w_up, L0_ffn_w_down):
    import jax
    import jax.numpy as jnp

    def _L0_xattn_ref(q, k, v, attention_mask, Wq, bq, Wk, bk, Wv, bv, Wo, bo):
        import jax, jax.numpy as jnp
        import numpy as np
        N_HEADS = 16
        D_MODEL = 512
        HEAD_DIM = D_MODEL // N_HEADS
        MASK_FILL = -100000000.0

        def _split_heads(x):
            B, S, _ = x.shape
            return x.reshape(B, S, N_HEADS, HEAD_DIM).transpose(0, 2, 1, 3)
        qm = _split_heads(q @ Wq.T + bq)
        km = _split_heads(k @ Wk.T + bk)
        vm = _split_heads(v @ Wv.T + bv)
        scores = jnp.einsum('bnlh,bnph->bnlp', qm, km) / np.sqrt(HEAD_DIM).astype(np.float32)
        mask = attention_mask[:, None, None, :]
        scores = jnp.where(mask, scores, MASK_FILL)
        attn = jax.nn.softmax(scores, axis=-1)
        out = jnp.einsum('bnlp,bnph->bnlh', attn, vm)
        B, _, L, _ = out.shape
        out = out.transpose(0, 2, 1, 3).reshape(B, L, D_MODEL)
        return out @ Wo.T + bo

    def _L0_attn_ref(x, Wq, Wk, Wv, Wo, bo):
        import jax, jax.numpy as jnp
        import numpy as np
        B, S, D = (2, 1024, 512)
        H, DH = (16, 64)
        SCALE = DH ** (-0.5)
        b, s, _ = x.shape
        q = (x @ Wq).reshape(b, s, H, DH)
        k = (x @ Wk).reshape(b, s, H, DH)
        v = (x @ Wv).reshape(b, s, H, DH)
        scores = jnp.einsum('bqhd,bkhd->bhqk', q, k) * SCALE
        attn = jax.nn.softmax(scores, axis=-1)
        out = jnp.einsum('bhqk,bkhd->bqhd', attn, v).reshape(b, s, H * DH)
        return out @ Wo + bo

    def _L0_ffn_ref(x, gate_w, w_gate, w_up, w_down):
        import jax, jax.numpy as jnp
        import numpy as np
        CAPACITY = 2
        B, S, D = x.shape
        E = gate_w.shape[0]
        k = S // E * CAPACITY
        logits = jnp.einsum('bsd,ed->bse', x, gate_w)
        affinity = jax.nn.softmax(logits, axis=-1)
        affinity = jnp.transpose(affinity, (0, 2, 1))
        gating, idx = jax.lax.top_k(affinity, k)
        bidx = jnp.arange(B)[:, None, None]
        x_in = x[bidx, idx]
        h = jax.nn.silu(jnp.einsum('bekd,eid->beki', x_in, w_gate)) * jnp.einsum('bekd,eid->beki', x_in, w_up)
        x_e = jnp.einsum('beki,edi->bekd', h, w_down)
        out = jnp.zeros_like(x).at[bidx, idx].add(gating[..., None] * x_e)
        return out
    x = x + _L0_xattn_ref(_layernorm(x, axis=-1), ctx_1024, ctx_1024, mask_BxS2_bf1, L0_xattn_Wq, L0_xattn_bq, L0_xattn_Wk, L0_xattn_bk, L0_xattn_Wv, L0_xattn_bv, L0_xattn_Wo, L0_xattn_bo)
    x = x + _L0_attn_ref(_layernorm(x, axis=-1), L0_attn_Wq, L0_attn_Wk, L0_attn_Wv, L0_attn_Wo, L0_attn_bo)
    x = x + _L0_ffn_ref(_layernorm(x, axis=-1), L0_ffn_gate_w, L0_ffn_w_gate, L0_ffn_w_up, L0_ffn_w_down)
    return x

_drawn_inputs = setup_inputs


def setup_inputs(seed=0):
    import zlib

    import numpy as np

    out = dict(_drawn_inputs(seed))
    spreads = {'L0_xattn_bq': (0.0, 0.334),
     'L0_xattn_bk': (0.0, 0.8),
     'L0_xattn_bv': (0.0, 0.1),
     'L0_xattn_bo': (0.0, 0.1),
     'L0_attn_bo': (0.0, 0.1)}
    factors = {'L0_attn_Wq': 8.0, 'L0_attn_Wk': 8.0}
    for name, (base, spread) in spreads.items():
        noise = np.random.default_rng([zlib.crc32(name.encode()), seed]).standard_normal(out[name].shape)
        drawn = base * np.exp(spread * noise) if base else spread * noise
        out[name] = jnp.asarray(drawn.astype(out[name].dtype))
    for name, factor in factors.items():
        out[name] = (out[name] * factor).astype(out[name].dtype)
    return out
```

```python
from contextlib import ExitStack

import concourse.bass as bass
from concourse import mybir
from concourse.alu_op_type import AluOpType as ALU

ACT = mybir.ActivationFunctionType
AX_X = mybir.AxisListType.X
F32 = mybir.dt.float32
F32R = mybir.dt.float32r
U8 = mybir.dt.uint8
U32 = mybir.dt.uint32

P = 128
BANK = 512
NB, S, D = 2, 512, 512
CTX = 8192
KT = D // P
ROWS = NB * S // P
QB = S // P
XH, XD = 16, 32
SH, SD = 16, 64
E, INNER = 8, 2048
CAP = S // E * 2
EPS = 1e-5
MASKED = 1e30


def semaphores(nc, ctx, prefix, names):
    return {n: ctx.enter_context(nc.semaphore(f"{prefix}_{n}")) for n in names.split()}


def buffers(nc, ctx, prefix, **shapes):
    return {n: ctx.enter_context(nc.sbuf_tensor(f"{prefix}_{n}", list(shape), dt)) for n, (shape, dt) in shapes.items()}


def words(ap):
    return ap.bitcast(F32)


def past(value):
    return not isinstance(value, int) or value > 0


def in_groups(engine, size, first, last, step):
    assert (last - first) % size == 0
    with engine.Fori(0, (last - first) // size) as i:
        for u in range(size):
            step(i * size + (first + u), i + (first + u) // size, (first + u) % size)


def in_pairs(engine, first, last, step):
    in_groups(engine, 2, first, last, step)


def load_residual(nc, g, ins):
    with ExitStack() as ctx:
        s = semaphores(nc, ctx, "load", "landed")
        block = ctx.enter_context(nc.Block())

        @block.sync
        def _(sp):
            sp.dma_start(g["x"][:], ins["x"].rearrange("(t p) d -> p t d", p=P)).then_inc(s["landed"], 16)
            sp.dma_start(g["ident"][:], ins["ident"]).then_inc(s["landed"], 16)
            sp.dma_start(g["fold"][:], ins["fold"]).then_inc(s["landed"], 16)
            sp.wait_ge(s["landed"], 48)


def normalise_rows(nc, g, tag, xT, keep=None):
    with ExitStack() as ctx:
        s = semaphores(nc, ctx, f"ln{tag}", "stats aggr var sd rstd rows turned")
        m = buffers(nc, ctx, f"ln{tag}", stats=([P, ROWS, 6], F32), mv=([P, ROWS, 2], F32), ve=([P, ROWS], F32),
                    sd=([P, ROWS], F32), rstd=([P, ROWS], F32), own=([P, ROWS, D], F32))
        rows = m["own"] if keep is None else keep
        block = ctx.enter_context(nc.Block())

        @block.vector
        def _(dve):
            for t in range(ROWS):
                nc.vector.bn_stats(m["stats"][:, t, :], g["x"][:, t, :]).then_inc(s["stats"], 1)
            for t in range(ROWS):
                dve.wait_ge(s["stats"], t + 1)
                nc.vector.bn_aggr(m["mv"][:, t, :], m["stats"][:, t, :]).then_inc(s["aggr"], 1)
            dve.wait_ge(s["aggr"], ROWS)
            nc.vector.tensor_scalar(m["ve"][:], m["mv"][:, :, 1], EPS, None, ALU.add).then_inc(s["var"], 1)
            dve.wait_ge(s["sd"], 1)
            nc.vector.reciprocal(m["rstd"][:], m["sd"][:]).then_inc(s["rstd"], 1)
            dve.wait_ge(s["rstd"], 1)
            for t in range(ROWS):
                nc.vector.tensor_scalar(rows[:, t, :], g["x"][:, t, :], m["mv"][:, t, 0:1], m["rstd"][:, t:t + 1],
                                        ALU.subtract, ALU.mult).then_inc(s["rows"], 1)

        @block.tensor
        def _(pe):
            for t in range(ROWS):
                pe.wait_ge(s["rows"], t + 1)
                for k in range(KT):
                    last = nc.tensor.transpose(g["ps"][:, t, k * P:(k + 1) * P], rows[:, t, k * P:(k + 1) * P], g["ident"][:])
                last.then_inc(s["turned"], 1)

        @block.scalar
        def _(act):
            act.wait_ge(s["var"], 1)
            nc.scalar.activation(m["sd"][:], m["ve"][:], ACT.Sqrt).then_inc(s["sd"], 1)
            for t in range(ROWS):
                act.wait_ge(s["turned"], t + 1)
                nc.scalar.copy(xT[:, :, t * P:(t + 1) * P], g["ps"][:, t, :].rearrange("p (k c) -> p k c", k=KT))


def cross_queries(nc, g, xT, ins, scr):
    with ExitStack() as ctx:
        s = semaphores(nc, ctx, "q", "landed mask bias prod full hi lo stored")
        m = buffers(nc, ctx, "q", w=([P, KT, D], F32), b=([P, KT], F32), full=([P, NB * KT, BANK], F32),
                    hi=([P, NB * KT, BANK], F32R), lo=([P, NB * KT, BANK], F32R),
                    mask=([P, P], U8), bias=([P, P], F32R))
        block = ctx.enter_context(nc.Block())

        @block.sync
        def _(sp):
            sp.dma_start(m["mask"][:], ins["mask"].rearrange("b (p c) -> (b p) c", c=P)).then_inc(s["mask"], 16)
            sp.dma_start(m["w"][:], ins["xWq"]).then_inc(s["landed"], 16)
            sp.dma_start(m["b"][:], ins["xbq"]).then_inc(s["landed"], 16)
            sp.wait_ge(s["bias"], 1)
            sp.dma_start(scr["maskbias"].rearrange("b (p c) -> (b p) c", c=P), words(m["bias"][:])).then_inc(s["stored"], 16)
            sp.wait_ge(s["hi"], NB * KT)
            for copy in range(2):
                sp.dma_start(scr["q"][copy].rearrange("(n p) c -> p n c", p=P), words(m["hi"][:])).then_inc(s["stored"], 16)
            sp.wait_ge(s["lo"], NB * KT)
            sp.dma_start(scr["q"][2].rearrange("(n p) c -> p n c", p=P), words(m["lo"][:])).then_inc(s["stored"], 16)
            sp.wait_ge(s["stored"], 64)

        @block.tensor
        def _(pe):
            pe.wait_ge(s["landed"], 32)
            for n in range(NB * KT):
                b, f = n // KT, n % KT
                for k in range(KT):
                    last = nc.tensor.matmul(g["ps"][:, n, :], m["w"][:, k, f * P:(f + 1) * P],
                                            xT[:, k, b * S:(b + 1) * S], start=(k == 0), stop=(k == KT - 1))
                last.then_inc(s["prod"], 1)

        @block.vector
        def _(dve):
            dve.wait_ge(s["mask"], 16)
            nc.vector.tensor_scalar(m["bias"][:], m["mask"][:], 1.0, MASKED, ALU.subtract, ALU.mult).then_inc(s["bias"], 1)
            for n in range(NB * KT):
                dve.wait_ge(s["prod"], n + 1)
                nc.vector.tensor_scalar(m["full"][:, n, :], g["ps"][:, n, :], m["b"][:, n % KT:n % KT + 1], None,
                                        ALU.add).then_inc(s["full"], 1)
                dve.wait_ge(s["hi"], n + 1)
                nc.vector.tensor_tensor(m["lo"][:, n, :], m["full"][:, n, :], m["hi"][:, n, :].bitcast(F32),
                                        ALU.subtract).then_inc(s["lo"], 1)

        @block.scalar
        def _(act):
            for n in range(NB * KT):
                act.wait_ge(s["full"], n + 1)
                nc.scalar.copy(m["hi"][:, n, :], m["full"][:, n, :]).then_inc(s["hi"], 1)


def project_context(nc, g, ins, scr):
    TILES = NB * CTX // BANK
    TPB = CTX // BANK
    NC4 = BANK // P
    with ExitStack() as ctx:
        s = semaphores(nc, ctx, "proj", "w whi wlo in0 in1 m0 m1 hi lo tile kprod kfull khi klo vprod vhi vlo ks0 ks1 vs0 vs1")
        raw_in, mask_in = (s["in0"], s["in1"]), (s["m0"], s["m1"])
        k_stored, v_stored = (s["ks0"], s["ks1"]), (s["vs0"], s["vs1"])
        m = buffers(nc, ctx, "proj", wk=([P, KT, D], F32), wv=([P, KT, D], F32), bk=([P, KT], F32),
                    wk_hi=([P, KT, D], F32R), wk_lo=([P, KT, D], F32R), wv_hi=([P, KT, D], F32R), wv_lo=([P, KT, D], F32R),
                    raw=([P, 2, KT, BANK], F32), hi=([P, 2, KT, BANK], F32R), lo=([P, 2, KT, BANK], F32R),
                    mask=([P, 2, BANK], U8), kfull=([P, 2, BANK], F32),
                    khi=([P, 2, KT, BANK], F32R), klo=([P, 2, KT, BANK], F32R),
                    v=([P, 2, XH, NC4, 2 * XD + 1], F32R))
        block = ctx.enter_context(nc.Block())

        @block.sync
        def _(sp):
            def load(j, par):
                sp.dma_start(m["raw"][:, par], ins["ctx"][j]).then_inc(raw_in[par], 16)
                sp.dma_start(m["mask"][:, par], ins["mask_tiles"][j].partition_broadcast(P)).then_inc(mask_in[par], 16)

            def step(j, half, par, more=True):
                sp.wait_ge(s["klo"], j * KT + KT)
                sp.dma_start(scr["k"][0, j].rearrange("(f p) c -> p f c", p=P), words(m["khi"][:, par])).then_inc(k_stored[par], 16)
                sp.dma_start(scr["k"][1, j].rearrange("(f p) c -> p f c", p=P), words(m["klo"][:, par])).then_inc(k_stored[par], 16)
                sp.wait_ge(s["vlo"], j * NC4 + NC4)
                sp.dma_start(scr["v"][j].rearrange("h p c -> p h c"),
                             words(m["v"][:, par].rearrange("p h c e -> p h (c e)"))).then_inc(v_stored[par], 16)
                if more:
                    load(j + 2, par)

            for name, src in ((m["wk"], ins["xWk"]), (m["wv"], ins["xWv"]), (m["bk"], ins["xbk"])):
                sp.dma_start(name[:], src).then_inc(s["w"], 16)
            load(0, 0)
            load(1, 1)
            in_pairs(sp, 0, TILES - 2, step)
            step(TILES - 2, TILES // 2 - 1, 0, more=False)
            step(TILES - 1, TILES // 2 - 1, 1, more=False)
            for q in k_stored:
                sp.wait_ge(q, 32 * TILES // 2)
            for q in v_stored:
                sp.wait_ge(q, 16 * TILES // 2)

        @block.tensor
        def _(pe):
            k_passes = ((m["wk_hi"], m["hi"]), (m["wk_hi"], m["lo"]), (m["wk_lo"], m["hi"]))
            v_passes = ((m["hi"], m["wv_hi"]), (m["lo"], m["wv_hi"]), (m["hi"], m["wv_lo"]))

            def step(j, half, par):
                pe.wait_ge(s["lo"], j + 1)
                for f in range(KT):
                    if past(j):
                        pe.wait_ge(s["kfull"], j * KT + (f + 1 - KT))
                    n = 0
                    for w, c in k_passes:
                        for k in range(KT):
                            last = nc.tensor.matmul(g["ps"][:, f, :], w[:, k, f * P:(f + 1) * P], c[:, par, k, :],
                                                    start=(n == 0), stop=(n == 3 * KT - 1))
                            n += 1
                    last.then_inc(s["kprod"], 1)
                for t in range(NC4):
                    if past(j):
                        pe.wait_ge(s["vlo"], j * NC4 + (t + 1 - NC4))
                    n = 0
                    for c, w in v_passes:
                        for k in range(KT):
                            last = nc.tensor.matmul(g["ps"][:, KT + t, :], c[:, par, k, t * P:(t + 1) * P], w[:, k, :],
                                                    start=(n == 0), stop=(n == 3 * KT - 1))
                            n += 1
                    last.then_inc(s["vprod"], 1)

            pe.wait_ge(s["wlo"], 2)
            step(0, 0, 0)
            step(1, 0, 1)
            in_pairs(pe, 2, TILES, step)

        def split_hi(act, j, half, par):
            act.wait_ge(raw_in[par], half * 16 + 16)
            if past(j * NC4 - NC4):
                act.wait_ge(s["vprod"], j * NC4 - NC4)
            nc.scalar.copy(m["hi"][:, par].rearrange("p k c -> p (k c)"),
                           m["raw"][:, par].rearrange("p k c -> p (k c)")).then_inc(s["hi"], 1)

        def split_lo(dve, j, par):
            dve.wait_ge(s["hi"], j + 1)
            nc.vector.tensor_tensor(m["lo"][:, par].rearrange("p k c -> p (k c)"),
                                    m["raw"][:, par].rearrange("p k c -> p (k c)"),
                                    m["hi"][:, par].rearrange("p k c -> p (k c)").bitcast(F32),
                                    ALU.subtract).then_inc(s["lo"], 1)

        @block.scalar
        def _(act):
            def step(j, half, par, more=True):
                if past(half):
                    act.wait_ge(k_stored[par], half * 32)
                for f in range(KT):
                    act.wait_ge(s["kfull"], j * KT + (f + 1))
                    nc.scalar.copy(m["khi"][:, par, f, :], m["kfull"][:, f % 2, :]).then_inc(s["khi"], 1)
                if more:
                    split_hi(act, j + 1, half + par, 1 - par)
                if past(half):
                    act.wait_ge(v_stored[par], half * 16)
                for t in range(NC4):
                    act.wait_ge(s["vprod"], j * NC4 + (t + 1))
                    nc.scalar.copy(m["v"][:, par, :, t, 0:XD], g["ps"][:, KT + t, :].rearrange("p (h d) -> p h d", h=XH)
                                   ).then_inc(s["vhi"], 1)

            act.wait_ge(s["w"], 48)
            for hi, w in ((m["wk_hi"], m["wk"]), (m["wv_hi"], m["wv"])):
                nc.scalar.copy(hi[:], w[:]).then_inc(s["whi"], 1)
            split_hi(act, 0, 0, 0)
            step(0, 0, 0)
            step(1, 0, 1)
            in_pairs(act, 2, TILES - 2, step)
            step(TILES - 2, TILES // 2 - 1, 0)
            step(TILES - 1, TILES // 2 - 1, 1, more=False)

        @block.vector
        def _(dve):
            def step(j, half, par, more=True):
                dve.wait_ge(mask_in[par], half * 16 + 16)
                if past(half):
                    dve.wait_ge(k_stored[par], half * 32)
                for f in range(KT):
                    dve.wait_ge(s["kprod"], j * KT + (f + 1))
                    if past(j * KT + (f - 1)):
                        dve.wait_ge(s["klo"], j * KT + (f - 1))
                    nc.vector.scalar_tensor_tensor(out=m["kfull"][:, f % 2, :], in0=g["ps"][:, f, :], scalar=m["bk"][:, f:f + 1],
                                                   in1=m["mask"][:, par, :], op0=ALU.add, op1=ALU.mult).then_inc(s["kfull"], 1)
                    dve.wait_ge(s["khi"], j * KT + (f + 1))
                    nc.vector.tensor_tensor(m["klo"][:, par, f, :], m["kfull"][:, f % 2, :],
                                            m["khi"][:, par, f, :].bitcast(F32), ALU.subtract).then_inc(s["klo"], 1)
                if more:
                    split_lo(dve, j + 1, 1 - par)
                if past(half):
                    dve.wait_ge(v_stored[par], half * 16)
                for t in range(NC4):
                    dve.wait_ge(s["vhi"], j * NC4 + (t + 1))
                    nc.vector.tensor_tensor(m["v"][:, par, :, t, XD:2 * XD], g["ps"][:, KT + t, :].rearrange("p (h d) -> p h d", h=XH),
                                            m["v"][:, par, :, t, 0:XD].bitcast(F32), ALU.subtract).then_inc(s["vlo"], 1)

            nc.vector.memset(words(m["v"][:, :, :, :, 2 * XD:]), 1.0)
            for n, (lo, w, hi) in enumerate(((m["wk_lo"], m["wk"], m["wk_hi"]), (m["wv_lo"], m["wv"], m["wv_hi"]))):
                dve.wait_ge(s["whi"], n + 1)
                nc.vector.tensor_tensor(lo[:], w[:], hi[:].bitcast(F32), ALU.subtract).then_inc(s["wlo"], 1)
            split_lo(dve, 0, 0)
            step(0, 0, 0)
            step(1, 0, 1)
            in_pairs(dve, 2, TILES - 2, step)
            step(TILES - 2, TILES // 2 - 1, 0)
            step(TILES - 1, TILES // 2 - 1, 1, more=False)


def cross_attention(nc, g, ins, scr):
    HEADS = NB * XH
    NG = CTX // (2 * P)
    RING = 4
    LAG = 2
    QUARTERS = 4
    KC = CTX // BANK
    TILES = KC * QB
    PER = TILES + 2
    OUT_G = LAG + 1
    ROW_G = NG - 2
    SCALE = float(XD) ** -0.5
    VW = 2 * XD + 1
    upto = [min(TILES, -(-TILES * (t + 1) // (ROW_G - 1))) for t in range(NG)]
    chunks = [range(upto[t - 1] if t else 0, upto[t]) for t in range(NG)]
    k_view = scr["k"].rearrange("s (b q t) (h r) c -> s b q h r t c", b=NB, q=QUARTERS, h=XH)
    v_view = scr["v"].rearrange("(b t) h p c -> b h p t c", b=NB)
    with ExitStack() as ctx:
        s = semaphores(nc, ctx, "xa", "ones scored p turned_p pv ring_in ring_out topped maxed row out_read inv "
                       "q0 q1 m0 m1 v0 v1 " + " ".join(f"k{par}{q}" for par in range(2) for q in range(QUARTERS)))
        q_in, qmax_in, v_in = (s["q0"], s["q1"]), (s["m0"], s["m1"]), (s["v0"], s["v1"])
        k_in = ((s["k00"], s["k01"], s["k02"], s["k03"]), (s["k10"], s["k11"], s["k12"], s["k13"]))
        m = buffers(nc, ctx, "xa", k=([P, 2, CTX], F32R), v=([P, 2, CTX // P, VW], F32R),
                    q=([P, 2, S], F32R), qmax=([P, 2, S], F32R),
                    full=([P, RING, 2 * BANK], F32), hi=([P, RING, 2 * BANK], F32R), lo=([P, RING, 2 * BANK], F32R),
                    mx=([P, QB, KC], F32), top=([P, QB], F32), row=([P, QB, 2], F32), o=([P, S], F32), den=([P, QB], F32))
        O, R = 4, 6
        block = ctx.enter_context(nc.Block())

        @block.sync
        def _(sp):
            def load_k(b, h, par, q):
                cols = slice(q * CTX // QUARTERS, (q + 1) * CTX // QUARTERS)
                for part, row in ((0, 0), (1, XD), (0, 2 * XD)):
                    sp.dma_start(words(m["k"][row:row + XD, par, cols].rearrange("r (t c) -> r t c", c=BANK)),
                                 k_view[part, b, q, h]).then_inc(k_in[par][q], 16)
                sp.dma_start(words(m["k"][3 * XD:3 * XD + 1, par, cols]),
                             scr["maskbias"][b:b + 1, cols] if isinstance(b, int) else scr["maskbias"][bass.ds(b, 1), cols]
                             ).then_inc(k_in[par][q], 16)

            def load_q(n, par, dst, sem):
                for part in range(3):
                    sp.dma_start(words(dst[part * XD:(part + 1) * XD, par, :]),
                                 scr["q"][part].rearrange("(n r) c -> n r c", r=XD)[n]).then_inc(sem[par], 16)

            def load_v(b, h, par):
                sp.dma_start(words(m["v"][:, par].rearrange("p (t c) e -> p t (c e)", c=BANK // P)), v_view[b, h]).then_inc(v_in[par], 16)

            def step(n, half, par, more=True):
                if past(n):
                    sp.wait_ge(s["scored"], n * NG)
                load_k((n + 1) // XH, (n + 1) % XH, 1 - par, QUARTERS - 1)
                load_q(n + 1, 1 - par, m["q"], q_in)
                if more:
                    sp.wait_ge(s["ring_in"], n * PER + TILES)
                    load_q(n + 2, par, m["qmax"], qmax_in)
                if past(n):
                    sp.wait_ge(s["pv"], n * NG)
                load_v((n + 1) // XH, (n + 1) % XH, 1 - par)
                if more:
                    for q in range(QUARTERS - 1):
                        sp.wait_ge(s["scored"], n * NG + (q + 1) * (NG // QUARTERS))
                        load_k((n + 2) // XH, (n + 2) % XH, par, q)

            sp.wait_ge(s["ones"], 1)
            load_q(0, 0, m["qmax"], qmax_in)
            for q in range(QUARTERS):
                load_k(0, 0, 0, q)
            load_q(0, 0, m["q"], q_in)
            load_v(0, 0, 0)
            load_q(1, 1, m["qmax"], qmax_in)
            for q in range(QUARTERS - 1):
                load_k(0, 1, 1, q)
            step(0, 0, 0)
            step(1, 0, 1)
            in_pairs(sp, 2, HEADS - 2, step)
            step(HEADS - 2, HEADS // 2 - 1, 0, more=False)

        def ring_base(n):
            return n * PER + TILES if not isinstance(n, int) or n > 0 else TILES + 1

        @block.tensor
        def _(pe):
            def ring_slot(entry, parity):
                if past(entry - 1):
                    pe.wait_ge(s["ring_out"], entry - 1)
                return g["ps"][:, R + parity, :]

            def max_product(half, par, idx, entry, parity):
                kc, qb = idx // QB, idx % QB
                if idx == 0:
                    pe.wait_ge(qmax_in[par], half * 48 + 48)
                if qb == 0 and kc % (KC // QUARTERS) == 0:
                    pe.wait_ge(k_in[par][kc // (KC // QUARTERS)], half * 64 + 64)
                out = ring_slot(entry, parity)
                nc.tensor.matmul(out, m["qmax"][0:3 * XD + 1, par, qb * P:(qb + 1) * P],
                                 m["k"][0:3 * XD + 1, par, kc * BANK:(kc + 1) * BANK], start=True, stop=True
                                 ).then_inc(s["ring_in"], 1)

            def turn_maxima(n, entry, parity):
                pe.wait_ge(s["maxed"], n + 1)
                out = ring_slot(entry, parity)
                for qb in range(QB):
                    last = nc.tensor.matmul(out[3 * XD:3 * XD + 2, qb * P:(qb + 1) * P], m["row"][:, qb, :], g["ident"][:],
                                            start=True, stop=True)
                last.then_inc(s["ring_in"], 1)

            def turn_output(n, entry, parity):
                pe.wait_ge(s["out_read"], n + 2)
                out = ring_slot(entry, parity)
                for qb in range(QB):
                    last = nc.tensor.matmul(out[:, qb * P:qb * P + XD + 1], m["o"][0:VW, qb * P:(qb + 1) * P], g["fold"][0:VW, :],
                                            start=True, stop=True)
                last.then_inc(s["ring_in"], 1)

            def values(n, half, par, t, group):
                if t == 0:
                    pe.wait_ge(v_in[par], half * 16 + 16)
                    if past(n):
                        pe.wait_ge(s["out_read"], n)
                pe.wait_ge(s["turned_p"], group + 1)
                for c in range(2):
                    for part in (m["hi"], m["lo"]):
                        last = nc.tensor.matmul(g["ps"][0:VW, O + par, :], m["v"][:, par, 2 * t + c, :],
                                                part[:, t % RING, c * BANK:(c + 1) * BANK],
                                                start=(t == 0 and c == 0 and part is m["hi"]),
                                                stop=(t == NG - 1 and c == 1 and part is m["lo"]))
                last.then_inc(s["pv"], 1)

            def step(n, half, par, maxima=True):
                entry, r = ring_base(n), (ring_base(n) % 2 if isinstance(n, int) else 0)
                first = isinstance(n, int) and n == 0
                for t in range(NG):
                    group = n * NG + t
                    if t == 0:
                        pe.wait_ge(q_in[par], half * 48 + 48)
                        pe.wait_ge(s["row"], n + 1)
                    if past(group - 1):
                        pe.wait_ge(s["p"], group - 1)
                    for c in range(2):
                        key = (2 * t + c) * P
                        last = nc.tensor.matmul(g["ps"][:, 2 * (t % 2) + c, :], m["k"][0:3 * XD + 2, par, key:key + P],
                                                m["q"][0:3 * XD + 2, par, :], start=True, stop=True)
                    last.then_inc(s["scored"], 1)
                    if maxima:
                        for idx in chunks[t]:
                            max_product(half + par, 1 - par, idx, entry, r % 2)
                            entry, r = entry + 1, r + 1
                        if t == ROW_G:
                            turn_maxima(n + 1, entry, r % 2)
                            entry, r = entry + 1, r + 1
                    if t == OUT_G and not first:
                        turn_output(n - 1, entry, r % 2)
                        entry, r = entry + 1, r + 1
                    if t >= LAG:
                        values(n, half, par, t - LAG, group - LAG)
                    elif not first:
                        values(n - 1, half + par - 1, 1 - par, NG - LAG + t, group - LAG)

            for idx in range(TILES):
                max_product(0, 0, idx, idx, idx % 2)
            turn_maxima(0, TILES, TILES % 2)
            step(0, 0, 0)
            in_pairs(pe, 1, HEADS - 1, step)
            n = HEADS - 1
            step(n, n // 2, n % 2, maxima=False)
            for t in range(NG - LAG, NG):
                values(n, n // 2, n % 2, t, n * NG + t + 0)
            turn_output(n, ring_base(n) + 1, (ring_base(n) + 1) % 2)

        @block.scalar
        def _(act):
            def step(n, half, par):
                for t in range(NG):
                    group = n * NG + t
                    act.wait_ge(s["scored"], group + 1)
                    if past(group + 1 - RING):
                        act.wait_ge(s["turned_p"], group + 1 - RING)
                    scores = g["ps"][:, 2 * (t % 2):2 * (t % 2) + 2, :].rearrange("p a c -> p (a c)")
                    nc.scalar.activation(m["full"][:, t % RING, :], scores, ACT.Exp, scale=SCALE)
                    if past(group + 1 - RING):
                        act.wait_ge(s["pv"], group + 1 - RING)
                    nc.scalar.activation(m["hi"][:, t % RING, :], scores, ACT.Exp, scale=SCALE).then_inc(s["p"], 1)

            step(0, 0, 0)
            in_pairs(act, 1, HEADS - 1, step)
            step(HEADS - 1, HEADS // 2 - 1, 1)

        @block.vector
        def _(dve):
            def read_max(idx, entry, parity):
                dve.wait_ge(s["ring_in"], entry + 1)
                kc, qb = idx // QB, idx % QB
                nc.vector.tensor_reduce(m["mx"][:, qb, kc:kc + 1], g["ps"][:, R + parity, :], AX_X, ALU.max
                                        ).then_inc(s["ring_out"], 1)

            def finish_maxima(n, entry):
                dve.wait_ge(s["ring_out"], entry)
                nc.vector.tensor_reduce(m["top"][:], m["mx"][:], AX_X, ALU.max).then_inc(s["topped"], 1)
                dve.wait_ge(s["topped"], n + 1)
                nc.vector.tensor_scalar(m["row"][:, :, 1], m["top"][:], -1.0, None, ALU.mult).then_inc(s["maxed"], 1)

            def read_row(n, half, par, entry, parity):
                dve.wait_ge(s["ring_in"], entry + 1)
                if past(n - 1):
                    dve.wait_ge(s["scored"], (n - 1) * NG)
                nc.vector.tensor_copy(m["q"][3 * XD:3 * XD + 2, par, :], g["ps"][3 * XD:3 * XD + 2, R + parity, :]
                                      ).then_inc(s["row"], 1)
                dve.wait_ge(s["row"], n + 1)
                dve.sem_inc(s["ring_out"], 1)

            def read_output(n, par):
                dve.wait_ge(s["pv"], (n + 1) * NG)
                nc.vector.tensor_copy(m["o"][0:VW, :], g["ps"][0:VW, O + par, :]).then_inc(s["out_read"], 1)

            def write_output(n, entry, parity):
                dve.wait_ge(s["ring_in"], entry + 1)
                out = g["ps"][:, R + parity, :].rearrange("p (q c) -> p q c", q=QB)
                nc.vector.reciprocal(m["den"][:], out[:, :, XD]).then_inc(s["inv"], 1)
                dve.wait_ge(s["inv"], n + 1)
                nc.vector.tensor_tensor(g["o"][:, n], out[:, :, 0:XD],
                                        m["den"][:].unsqueeze(2).to_broadcast([P, QB, XD]), ALU.mult).then_inc(s["ring_out"], 1)

            def low_part(t, group):
                dve.wait_ge(s["p"], group + 1)
                if past(group + 1 - RING):
                    dve.wait_ge(s["pv"], group + 1 - RING)
                nc.vector.tensor_tensor(m["lo"][:, t % RING, :], m["full"][:, t % RING, :],
                                        m["hi"][:, t % RING, :].bitcast(F32), ALU.subtract).then_inc(s["turned_p"], 1)

            def step(n, half, par, maxima=True):
                entry, r = ring_base(n), (ring_base(n) % 2 if isinstance(n, int) else 0)
                first = isinstance(n, int) and n == 0
                for t in range(NG):
                    if maxima:
                        for idx in chunks[t]:
                            read_max(idx, entry, r % 2)
                            entry, r = entry + 1, r + 1
                            if idx == TILES - 1:
                                finish_maxima(n + 1, entry)
                        if t == ROW_G:
                            read_row(n + 1, half + par, 1 - par, entry, r % 2)
                            entry, r = entry + 1, r + 1
                    if t == OUT_G and not first:
                        write_output(n - 1, entry, r % 2)
                        entry, r = entry + 1, r + 1
                    low_part(t, n * NG + t)
                    if t == LAG and not first:
                        read_output(n - 1, 1 - par)

            dve.sem_inc(s["out_read"], 1)
            nc.vector.memset(m["row"][:], 1.0)
            nc.vector.memset(words(m["q"][3 * XD:3 * XD + 2]), 1.0)
            nc.vector.memset(words(m["qmax"][3 * XD:3 * XD + 2]), 1.0)
            nc.vector.memset(words(m["k"][3 * XD:3 * XD + 2]), 1.0).then_inc(s["ones"], 1)
            dve.wait_ge(s["ones"], 1)
            for idx in range(TILES):
                read_max(idx, idx, idx % 2)
            finish_maxima(0, TILES)
            read_row(0, 0, 0, TILES, TILES % 2)
            step(0, 0, 0)
            in_pairs(dve, 1, HEADS - 1, step)
            n = HEADS - 1
            step(n, n // 2, n % 2, maxima=False)
            read_output(n, n % 2)
            write_output(n, ring_base(n) + 1, (ring_base(n) + 1) % 2)


def output_projection(nc, g, tag, rows, width, w_in, bias_in, add=None):
    KW = width // P
    with ExitStack() as ctx:
        s = semaphores(nc, ctx, f"out{tag}", "landed rows turned copied prod added done")
        m = buffers(nc, ctx, f"out{tag}", w=([P, KW, D], F32), bias=([P, D], F32), add=([P, width], F32),
                    rows=([P, 2, width], F32), turned=([P, 2, KW, P], F32))
        T, Y = 0, 4
        block = ctx.enter_context(nc.Block())

        @block.sync
        def _(sp):
            sp.dma_start(m["w"][:], w_in).then_inc(s["landed"], 16)
            sp.dma_start(m["bias"][:], bias_in.partition_broadcast(P)).then_inc(s["landed"], 16)
            if add is not None:
                sp.dma_start(m["add"][:], add.partition_broadcast(P)).then_inc(s["landed"], 16)
            sp.wait_ge(s["landed"], 32 if add is None else 48)

        def bank_of(t, k):
            return g["ps"][:, T + 2 * (t % 2) + k // 4, (k % 4) * P:(k % 4 + 1) * P]

        @block.vector
        def _(dve):
            def accumulate(t):
                dve.wait_ge(s["prod"], t + 1)
                nc.vector.tensor_tensor(g["x"][:, t, :], g["ps"][:, Y + t % 2, :], g["x"][:, t, :], ALU.add).then_inc(s["added"], 1)
                dve.wait_ge(s["added"], t + 1)
                nc.vector.tensor_tensor(g["x"][:, t, :], g["x"][:, t, :], m["bias"][:], ALU.add).then_inc(s["done"], 1)

            dve.wait_ge(s["landed"], 32 if add is None else 48)
            for t in range(ROWS):
                if t >= 2:
                    dve.wait_ge(s["turned"], t - 1)
                out = m["rows"][:, t % 2, :]
                if add is None:
                    nc.vector.tensor_copy(out, rows(t)).then_inc(s["rows"], 1)
                else:
                    nc.vector.tensor_tensor(out.rearrange("p (h d) -> p h d", d=XD), rows(t),
                                            m["add"][:].rearrange("p (h d) -> p h d", d=XD), ALU.add).then_inc(s["rows"], 1)
                if t:
                    accumulate(t - 1)
            accumulate(ROWS - 1)

        @block.scalar
        def _(act):
            for t in range(ROWS):
                act.wait_ge(s["turned"], t + 1)
                if t >= 2:
                    act.wait_ge(s["prod"], t - 1)
                for half in range(-(-KW // 4)):
                    last = nc.scalar.copy(m["turned"][:, t % 2, 4 * half:4 * half + 4].rearrange("p k c -> p (k c)"),
                                          g["ps"][:, T + 2 * (t % 2) + half, :])
                last.then_inc(s["copied"], 1)

        @block.tensor
        def _(pe):
            pe.wait_ge(s["landed"], 32 if add is None else 48)
            for t in range(ROWS):
                pe.wait_ge(s["rows"], t + 1)
                if t >= 2:
                    pe.wait_ge(s["copied"], t - 1)
                for k in range(KW):
                    last = nc.tensor.transpose(bank_of(t, k), m["rows"][:, t % 2, k * P:(k + 1) * P], g["ident"][:])
                last.then_inc(s["turned"], 1)
                pe.wait_ge(s["copied"], t + 1)
                if t >= 2:
                    pe.wait_ge(s["added"], t - 1)
                for k in range(KW):
                    last = nc.tensor.matmul(g["ps"][:, Y + t % 2, :], m["turned"][:, t % 2, k, :], m["w"][:, k, :],
                                            start=(k == 0), stop=(k == KW - 1))
                last.then_inc(s["prod"], 1)


def self_projections(nc, g, xT, ins, scr, v):
    FT = SH * SD // P
    OUTS = NB * FT
    VOUT = ROWS * SH * SD // BANK
    with ExitStack() as ctx:
        s = semaphores(nc, ctx, "sp", "w whi wlo xhi xlo prod hi lo vread st0 st1 st2 st3")
        stored = (s["st0"], s["st1"], s["st2"], s["st3"])
        m = buffers(nc, ctx, "sp", w=([P, KT, SH * SD], F32), x_hi=([P, KT, NB * S], F32R), x_lo=([P, KT, NB * S], F32R),
                    w_hi=([P, KT, SH * SD], F32R), w_lo=([P, KT, SH * SD], F32R),
                    hi=([P, 4, BANK], F32R), lo=([P, 4, BANK], F32R))
        block = ctx.enter_context(nc.Block())
        WEIGHTS = (ins["sWq"], ins["sWk"], ins["sWv"])
        BANKS = 8

        @block.sync
        def _(sp):
            for i, w in enumerate(WEIGHTS):
                if i:
                    sp.wait_ge(s["wlo"], i)
                sp.dma_start(m["w"][:], w).then_inc(s["w"], 16)
                if i < 2:
                    dst = (scr["sq"], scr["sk"])[i]
                    for n in range(OUTS):
                        o = i * OUTS + n
                        rows = slice(n % FT * P, (n % FT + 1) * P)
                        sp.wait_ge(s["lo"], o + 1)
                        sp.dma_start(dst[0, n // FT, rows], words(m["hi"][:, o % 4])).then_inc(stored[o % 4], 16)
                        sp.dma_start(dst[1, n // FT, rows], words(m["lo"][:, o % 4])).then_inc(stored[o % 4], 16)
            for q in stored:
                sp.wait_ge(q, 32 * 2 * OUTS // 4)

        @block.tensor
        def _(pe):
            for o in range(2 * OUTS + VOUT):
                i, n = min(o // OUTS, 2), o if o < OUTS else (o - OUTS if o < 2 * OUTS else o - 2 * OUTS)
                if n == 0:
                    pe.wait_ge(s["wlo"], i + 1)
                    pe.wait_ge(s["xlo"], 1)
                if o >= BANKS:
                    if o - BANKS < 2 * OUTS:
                        pe.wait_ge(s["lo"], o - BANKS + 1)
                    else:
                        pe.wait_ge(s["vread"], o - BANKS - 2 * OUTS + 1)
                count = 0
                for x, w in ((m["x_hi"], m["w_hi"]), (m["x_lo"], m["w_hi"]), (m["x_hi"], m["w_lo"])):
                    for k in range(KT):
                        if i < 2:
                            lhsT, rhs = w[:, k, n % FT * P:(n % FT + 1) * P], x[:, k, n // FT * S:(n // FT + 1) * S]
                        else:
                            lhsT, rhs = x[:, k, n // 2 * P:(n // 2 + 1) * P], w[:, k, n % 2 * BANK:(n % 2 + 1) * BANK]
                        last = nc.tensor.matmul(g["ps"][:, o % BANKS, :], lhsT, rhs, start=(count == 0), stop=(count == 3 * KT - 1))
                        count += 1
                last.then_inc(s["prod"], 1)

        @block.scalar
        def _(act):
            def split_weights(i):
                act.wait_ge(s["w"], 16 * i + 16)
                if i:
                    act.wait_ge(s["prod"], i * OUTS)
                nc.scalar.copy(m["w_hi"][:], m["w"][:]).then_inc(s["whi"], 1)

            nc.scalar.copy(m["x_hi"][:], xT[:]).then_inc(s["xhi"], 1)
            for i in range(3):
                split_weights(i)
                for o in range(i * OUTS, (i + 1) * OUTS if i < 2 else 0):
                    act.wait_ge(s["prod"], o + 1)
                    if o >= 4:
                        act.wait_ge(stored[o % 4], 32 * (o // 4))
                    nc.scalar.copy(m["hi"][:, o % 4], g["ps"][:, o % BANKS, :]).then_inc(s["hi"], 1)

        @block.vector
        def _(dve):
            nc.vector.memset(v[:, :, :, SD:], 1.0)
            dve.wait_ge(s["xhi"], 1)
            nc.vector.tensor_tensor(m["x_lo"][:], xT[:], m["x_hi"][:].bitcast(F32), ALU.subtract).then_inc(s["xlo"], 1)
            for i in range(3):
                dve.wait_ge(s["whi"], i + 1)
                nc.vector.tensor_tensor(m["w_lo"][:], m["w"][:], m["w_hi"][:].bitcast(F32), ALU.subtract).then_inc(s["wlo"], 1)
                for o in range(i * OUTS, (i + 1) * OUTS if i < 2 else 0):
                    dve.wait_ge(s["hi"], o + 1)
                    nc.vector.tensor_tensor(m["lo"][:, o % 4], g["ps"][:, o % BANKS, :], m["hi"][:, o % 4].bitcast(F32),
                                            ALU.subtract).then_inc(s["lo"], 1)
            for n in range(VOUT):
                dve.wait_ge(s["prod"], 2 * OUTS + n + 1)
                nc.vector.tensor_copy(v[:, n // 2, n % 2 * (SH // 2):(n % 2 + 1) * (SH // 2), 0:SD],
                                      g["ps"][:, (2 * OUTS + n) % BANKS, :].rearrange("p (h d) -> p h d", d=SD)
                                      ).then_inc(s["vread"], 1)


def self_attention(nc, g, ins, scr, v, out):
    HEADS = NB * SH
    NG = S // (2 * P)
    BUFS = 4
    VW = SD + 1
    SCALE = float(SD) ** -0.5
    PER = QB + 2
    with ExitStack() as ctx:
        s = semaphores(nc, ctx, "sa", "ones head_v scored p pv ring_in ring_out topped maxed row out_read inv in0 in1 in2 in3")
        landed = (s["in0"], s["in1"], s["in2"], s["in3"])
        m = buffers(nc, ctx, "sa", q1=([P, BUFS, S], F32R), q2=([P, BUFS, S], F32R), k1=([P, BUFS, S], F32R), k2=([P, BUFS, S], F32R),
                    v=([P, BUFS, QB, VW], F32), p=([P, 2 * NG, 2 * BANK], F32), mx=([P, QB], F32), row=([P, QB], F32),
                    o=([P, S], F32), den=([P, QB], F32))
        O, R = 4, 6
        block = ctx.enter_context(nc.Block())

        @block.sync
        def _(sp):
            def load(n, buf):
                q, k = (t.rearrange("s b (h r) c -> s b h r c", h=SH) for t in (scr["sq"], scr["sk"]))
                b, h = n // SH, n % SH
                for dst, row, src in ((m["q1"], 0, q[0]), (m["q1"], SD, q[0]), (m["q2"], 0, q[1]),
                                      (m["k1"], 0, k[0]), (m["k1"], SD, k[1]), (m["k2"], 0, k[0])):
                    sp.dma_start(words(dst[row:row + SD, buf]), src[b, h]).then_inc(landed[buf], 16)

            def step(n, turn, buf):
                if past(n):
                    sp.wait_ge(s["scored"], n * NG)
                load(n + 3, (buf + 3) % BUFS)

            sp.wait_ge(s["ones"], 1)
            for n in range(3):
                load(n, n)
            step(0, 0, 0)
            in_groups(sp, 4, 1, HEADS - 3, step)

        @block.gpsimd
        def _(pool):
            v_of = v.rearrange("p (b q) h c -> p b h q c", b=NB)

            def step(n, turn, buf):
                if past(n - 3):
                    pool.wait_ge(s["pv"], (n - 3) * NG)
                nc.gpsimd.tensor_copy(m["v"][:, buf], v_of[:, n // SH, n % SH]).then_inc(s["head_v"], 1)

            for n in range(4):
                step(n, 0, n)
            in_groups(pool, 4, 4, HEADS, step)

        def ring_base(n):
            return n * PER + 3 if not isinstance(n, int) or n >= 2 else (n + 1) * (PER - 1)

        def ring_parity(n):
            return ring_base(n) % 2 if isinstance(n, int) else 1

        @block.tensor
        def _(pe):
            def ring_slot(entry, parity):
                if past(entry - 1):
                    pe.wait_ge(s["ring_out"], entry - 1)
                return g["ps"][:, R + parity, :]

            def max_product(turn, buf, qb, entry, parity):
                if qb == 0:
                    pe.wait_ge(landed[buf], turn * 96 + 96)
                nc.tensor.matmul(ring_slot(entry, parity), m["q1"][:, buf, qb * P:(qb + 1) * P], m["k1"][:, buf, :],
                                 start=True, stop=True).then_inc(s["ring_in"], 1)

            def turn_maxima(n, entry, parity):
                pe.wait_ge(s["maxed"], n + 1)
                out = ring_slot(entry, parity)
                for qb in range(QB):
                    last = nc.tensor.matmul(out[SD:SD + 1, qb * P:(qb + 1) * P], m["row"][:, qb:qb + 1], g["ident"][:],
                                            start=True, stop=True)
                last.then_inc(s["ring_in"], 1)

            def turn_output(n, entry, parity):
                pe.wait_ge(s["out_read"], n + 2)
                out = ring_slot(entry, parity)
                for qb in range(QB):
                    last = nc.tensor.matmul(out[:, qb * P:qb * P + VW], m["o"][0:VW, qb * P:(qb + 1) * P], g["ident"][0:VW, 0:VW],
                                            start=True, stop=True)
                last.then_inc(s["ring_in"], 1)

            def values(n, buf, par, t):
                if t == 0:
                    pe.wait_ge(s["head_v"], n + 1)
                    if past(n):
                        pe.wait_ge(s["out_read"], n)
                pe.wait_ge(s["p"], n * NG + (t + 1))
                for c in range(2):
                    last = nc.tensor.matmul(g["ps"][0:VW, O + par, :], m["v"][:, buf, 2 * t + c, :],
                                            m["p"][:, par * NG + t, c * BANK:(c + 1) * BANK],
                                            start=(t == 0 and c == 0), stop=(t == NG - 1 and c == 1))
                last.then_inc(s["pv"], 1)

            def step(n, turn, buf, maxima=True):
                entry, r = ring_base(n), ring_parity(n)
                known = n if isinstance(n, int) else 2
                for t in range(NG):
                    if t == 0:
                        pe.wait_ge(s["row"], n + 1)
                    if past(n * NG + (t - 1)):
                        pe.wait_ge(s["p"], n * NG + (t - 1))
                    for c in range(2):
                        key = slice((2 * t + c) * P, (2 * t + c + 1) * P)
                        nc.tensor.matmul(g["ps"][:, 2 * t + c, :], m["k1"][:, buf, key], m["q1"][:, buf, :], start=True, stop=False)
                        last = nc.tensor.matmul(g["ps"][:, 2 * t + c, :], m["k2"][0:SD + 1, buf, key], m["q2"][0:SD + 1, buf, :],
                                                start=False, stop=True)
                    last.then_inc(s["scored"], 1)
                    if maxima:
                        for qb in (2 * t, 2 * t + 1):
                            max_product(turn + (buf + 1) // BUFS, (buf + 1) % BUFS, qb, entry, r % 2)
                            entry, r = entry + 1, r + 1
                    if known >= 1:
                        values(n - 1, (buf - 1) % BUFS, (buf - 1) % 2, t)
                    if t == 0 and known >= 2:
                        turn_output(n - 2, entry, r % 2)
                        entry, r = entry + 1, r + 1
                if maxima:
                    turn_maxima(n + 1, entry, r % 2)

            for qb in range(QB):
                max_product(0, 0, qb, qb, qb % 2)
            turn_maxima(0, QB, QB % 2)
            step(0, 0, 0)
            step(1, 0, 1)
            in_groups(pe, 4, 2, HEADS - 2, step)
            step(HEADS - 2, (HEADS - 2) // 4, (HEADS - 2) % 4)
            n = HEADS - 1
            step(n, n // 4, n % 4, maxima=False)
            for t in range(NG):
                values(n, n % 4, n % 2, t)
            entry = ring_base(n) + 1
            turn_output(n - 1, entry, entry % 2)
            turn_output(n, entry + 1, (entry + 1) % 2)

        @block.scalar
        def _(act):
            def step(n, turn, par):
                for t in range(NG):
                    act.wait_ge(s["scored"], n * NG + (t + 1))
                    if past(n - 1):
                        act.wait_ge(s["pv"], (n - 1) * NG)
                    nc.scalar.activation(m["p"][:, par * NG + t, :], g["ps"][:, 2 * t:2 * t + 2, :].rearrange("p a c -> p (a c)"),
                                         ACT.Exp, scale=SCALE).then_inc(s["p"], 1)

            step(0, 0, 0)
            step(1, 0, 1)
            in_pairs(act, 2, HEADS, step)

        @block.vector
        def _(dve):
            def read_max(qb, entry, parity):
                dve.wait_ge(s["ring_in"], entry + 1)
                nc.vector.tensor_reduce(m["mx"][:, qb:qb + 1], g["ps"][:, R + parity, :], AX_X, ALU.max).then_inc(s["ring_out"], 1)

            def finish_maxima(n, turn, buf, entry, parity):
                dve.wait_ge(s["ring_out"], entry)
                nc.vector.tensor_scalar(m["row"][:], m["mx"][:], -1.0, None, ALU.mult).then_inc(s["maxed"], 1)
                dve.wait_ge(s["ring_in"], entry + 1)
                nc.vector.tensor_copy(m["q2"][SD:SD + 1, buf, :], g["ps"][SD:SD + 1, R + parity, :]).then_inc(s["row"], 1)
                dve.wait_ge(s["row"], n + 1)
                dve.sem_inc(s["ring_out"], 1)

            def read_output(n, par):
                dve.wait_ge(s["pv"], (n + 1) * NG)
                nc.vector.tensor_copy(m["o"][0:VW, :], g["ps"][0:VW, O + par, :]).then_inc(s["out_read"], 1)

            def write_output(n, entry, parity):
                dve.wait_ge(s["ring_in"], entry + 1)
                turned = g["ps"][:, R + parity, :].rearrange("p (q c) -> p q c", q=QB)
                nc.vector.reciprocal(m["den"][:], turned[:, :, SD]).then_inc(s["inv"], 1)
                dve.wait_ge(s["inv"], n + 1)
                nc.vector.tensor_tensor(out.rearrange("p (b q) h d -> p b h q d", b=NB)[:, n // SH, n % SH],
                                        turned[:, :, 0:SD], m["den"][:].unsqueeze(2).to_broadcast([P, QB, SD]),
                                        ALU.mult).then_inc(s["ring_out"], 1)

            def step(n, turn, buf, maxima=True):
                entry, r = ring_base(n), ring_parity(n)
                known = n if isinstance(n, int) else 2
                if known >= 2:
                    read_output(n - 2, buf % 2)
                for t in range(NG):
                    if maxima:
                        for qb in (2 * t, 2 * t + 1):
                            read_max(qb, entry, r % 2)
                            entry, r = entry + 1, r + 1
                    if t == 0 and known >= 2:
                        write_output(n - 2, entry, r % 2)
                        entry, r = entry + 1, r + 1
                if maxima:
                    finish_maxima(n + 1, turn, (buf + 1) % BUFS, entry, r % 2)

            dve.sem_inc(s["out_read"], 1)
            nc.vector.memset(words(m["k2"][SD:SD + 1]), 1.0).then_inc(s["ones"], 1)
            dve.wait_ge(s["ones"], 1)
            for qb in range(QB):
                read_max(qb, qb, qb % 2)
            finish_maxima(0, 0, 0, QB, QB % 2)
            step(0, 0, 0)
            step(1, 0, 1)
            in_groups(dve, 4, 2, HEADS - 2, step)
            step(HEADS - 2, (HEADS - 2) // 4, (HEADS - 2) % 4)
            n = HEADS - 1
            step(n, n // 4, n % 4, maxima=False)
            entry = ring_base(n) + 1
            read_output(n - 1, (n - 1) % 2)
            write_output(n - 1, entry, entry % 2)
            read_output(n, n % 2)
            write_output(n, entry + 1, (entry + 1) % 2)


def route(nc, g, xT, ins, sel, scat, gate):
    PAIRS = NB * E
    TOP = 8
    NEG = -3.0e38
    with ExitStack() as ctx:
        s = semaphores(nc, ctx, "rt", "landed logits prob exped turned aff top turned2 cols spread sel done")
        m = buffers(nc, ctx, "rt", gw=([P, KT, E], F32), tok_row=([P, S], F32), tok_col=([P, QB], F32),
                    mx=([P, ROWS], F32), p=([P, ROWS, E], F32), sum=([P, ROWS], F32), aff=([PAIRS, 2, S], F32),
                    val=([PAIRS, CAP], F32), idx=([PAIRS, CAP], U32), idxf=([PAIRS, CAP], F32), idx_col=([P, PAIRS], F32))
        block = ctx.enter_context(nc.Block())

        @block.sync
        def _(sp):
            for dst, src in ((m["gw"], ins["gate_w"]), (m["tok_row"], ins["tok_row"]), (m["tok_col"], ins["tok_col"])):
                sp.dma_start(dst[:], src).then_inc(s["landed"], 16)

        @block.tensor
        def _(pe):
            pe.wait_ge(s["landed"], 48)
            for t in range(ROWS):
                at = (t % QB * NB + t // QB) * E
                for k in range(KT):
                    last = nc.tensor.matmul(g["ps"][:, 0, at:at + E], xT[:, k, t * P:(t + 1) * P], m["gw"][:, k, :],
                                            start=(k == 0), stop=(k == KT - 1))
            last.then_inc(s["logits"], 1)
            pe.wait_ge(s["aff"], 1)
            for q in range(QB):
                last = nc.tensor.transpose(g["ps"][0:PAIRS, 1, q * P:(q + 1) * P], m["p"][:, q * NB:(q + 1) * NB, :].rearrange("p b e -> p (b e)"), g["ident"][:])
            last.then_inc(s["turned"], 1)
            pe.wait_ge(s["done"], 1)
            nc.tensor.transpose(g["ps"][:, 2, 0:PAIRS], m["val"][:], g["ident"][0:PAIRS, 0:PAIRS])
            nc.tensor.transpose(g["ps"][:, 2, PAIRS:2 * PAIRS], m["idxf"][:], g["ident"][0:PAIRS, 0:PAIRS]).then_inc(s["turned2"], 1)
            for r in range(PAIRS):
                last = nc.tensor.matmul(g["ps"][:, 4 + r // 4, r % 4 * P:(r % 4 + 1) * P],
                                        g["ident"][0:PAIRS, r:r + 1].to_broadcast([PAIRS, P]), m["idxf"][:], start=True, stop=True)
            last.then_inc(s["spread"], 1)

        @block.scalar
        def _(act):
            act.wait_ge(s["prob"], 2)
            nc.scalar.activation(m["p"][:], m["p"][:], ACT.Exp).then_inc(s["exped"], 1)

        @block.vector
        def _(dve):
            dve.wait_ge(s["logits"], 1)
            logits = g["ps"][:, 0, 0:ROWS * E].rearrange("p (t e) -> p t e", e=E)
            nc.vector.tensor_reduce(m["mx"][:], logits, AX_X, ALU.max).then_inc(s["prob"], 1)
            dve.wait_ge(s["prob"], 1)
            nc.vector.tensor_tensor(m["p"][:], logits, m["mx"][:].unsqueeze(2).to_broadcast([P, ROWS, E]),
                                    ALU.subtract).then_inc(s["prob"], 1)
            dve.wait_ge(s["exped"], 1)
            nc.vector.tensor_reduce(m["sum"][:], m["p"][:], AX_X, ALU.add).then_inc(s["prob"], 1)
            dve.wait_ge(s["prob"], 3)
            nc.vector.reciprocal(m["mx"][:], m["sum"][:]).then_inc(s["prob"], 1)
            dve.wait_ge(s["prob"], 4)
            nc.vector.tensor_tensor(m["p"][:], m["p"][:], m["mx"][:].unsqueeze(2).to_broadcast([P, ROWS, E]), ALU.mult).then_inc(s["aff"], 1)
            dve.wait_ge(s["turned"], 1)
            nc.vector.tensor_copy(m["aff"][:, 0, :], g["ps"][0:PAIRS, 1, :]).then_inc(s["top"], 1)
            for r in range(CAP // TOP):
                best = m["val"][:, r * TOP:(r + 1) * TOP]
                dve.wait_ge(s["top"], 3 * r + 1)
                nc.vector.max(best, m["aff"][:, r % 2, :]).then_inc(s["top"], 1)
                dve.wait_ge(s["top"], 3 * r + 2)
                nc.vector.max_index(m["idx"][:, r * TOP:(r + 1) * TOP], best, m["aff"][:, r % 2, :]).then_inc(s["top"], 1)
                dve.wait_ge(s["top"], 3 * r + 3)
                nc.vector.match_replace(m["aff"][:, 1 - r % 2, :], best, m["aff"][:, r % 2, :], NEG).then_inc(s["top"], 1)
            dve.wait_ge(s["top"], 3 * (CAP // TOP) + 1)
            nc.vector.tensor_copy(m["idxf"][:], m["idx"][:]).then_inc(s["done"], 1)
            dve.wait_ge(s["turned2"], 1)
            nc.vector.tensor_copy(gate[:], g["ps"][:, 2, 0:PAIRS])
            nc.vector.tensor_copy(m["idx_col"][:], g["ps"][:, 2, PAIRS:2 * PAIRS]).then_inc(s["cols"], 1)
            dve.wait_ge(s["cols"], 1)
            for r in range(PAIRS):
                nc.vector.tensor_scalar(scat[:, r, :], m["tok_row"][:], m["idx_col"][:, r:r + 1], None, ALU.is_equal)
            dve.wait_ge(s["spread"], 1)
            for b in range(NB):
                spread = g["ps"][:, 4 + 2 * b:6 + 2 * b, :].rearrange("p a c -> p (a c)")
                for q in range(QB):
                    nc.vector.tensor_scalar(sel[:, b, q, :], spread, m["tok_col"][:, q:q + 1], None, ALU.is_equal)


def gather(nc, g, rows, sel, xin):
    OUTS = NB * KT * 2
    with ExitStack() as ctx:
        s = semaphores(nc, ctx, "ga", "hi lo prod read")
        m = buffers(nc, ctx, "ga", hi=([P, ROWS, D], F32R), lo=([P, ROWS, D], F32R))
        block = ctx.enter_context(nc.Block())

        @block.scalar
        def _(act):
            nc.scalar.copy(m["hi"][:], rows[:]).then_inc(s["hi"], 1)

        @block.tensor
        def _(pe):
            pe.wait_ge(s["lo"], 1)
            for n in range(OUTS):
                b, k, half = n // (KT * 2), n // 2 % KT, n % 2
                if n >= 8:
                    pe.wait_ge(s["read"], n - 7)
                count = 0
                for part in (m["hi"], m["lo"]):
                    for q in range(QB):
                        last = nc.tensor.matmul(g["ps"][:, n % 8, :], part[:, b * QB + q, k * P:(k + 1) * P],
                                                sel[:, b, q, half * BANK:(half + 1) * BANK],
                                                start=(count == 0), stop=(count == 2 * QB - 1))
                        count += 1
                last.then_inc(s["prod"], 1)

        @block.vector
        def _(dve):
            dve.wait_ge(s["hi"], 1)
            nc.vector.tensor_tensor(m["lo"][:], rows[:], m["hi"][:].bitcast(F32), ALU.subtract).then_inc(s["lo"], 1)
            for n in range(OUTS):
                b, k, half = n // (KT * 2), n // 2 % KT, n % 2
                dve.wait_ge(s["prod"], n + 1)
                nc.vector.tensor_copy(xin[:, k, half * (E // 2):(half + 1) * (E // 2), b, :],
                                      g["ps"][:, n % 8, :].rearrange("p (e c) -> p e c", c=CAP)).then_inc(s["read"], 1)


def experts(nc, g, ins, xin, gate, y_hi, y_lo):
    CHUNKS = INNER // BANK
    IT = BANK // P
    TOK = NB * CAP
    TILES = CHUNKS * IT
    LAG = 2
    HRING = 4
    with ExitStack() as ctx:
        s = semaphores(nc, ctx, "ex", "w0 w1 hidden exped plus inv silu h down yprod gcol yfull yhi ylo")
        w_in = (s["w0"], s["w1"])
        m = buffers(nc, ctx, "ex", wg=([P, 2, KT, BANK], F32), wu=([P, 2, KT, BANK], F32), wd=([P, 2, IT, D], F32),
                    e=([P, 2, TOK], F32), r=([P, 2, TOK], F32), si=([P, 2, TOK], F32), h=([P, HRING, TOK], F32),
                    gcol=([P, NB], F32), y=([P, NB, D], F32))
        Y = 4
        block = ctx.enter_context(nc.Block())

        @block.sync
        def _(sp):
            def load(e, c, buf):
                for dst, src in ((m["wg"], ins["w_gate"]), (m["wu"], ins["w_up"]), (m["wd"], ins["w_down"])):
                    sp.dma_start(dst[:, buf], src[e, c]).then_inc(w_in[buf], 16)

            def step(e, more=True):
                for c in range(CHUNKS):
                    if c < CHUNKS - 2 or more:
                        sp.wait_ge(s["down"], e * TILES + (c + 1) * IT)
                        load(e + (c + 2) // CHUNKS, (c + 2) % CHUNKS, c % 2)

            load(0, 0, 0)
            load(0, 1, 1)
            with sp.Fori(0, E - 1) as e:
                step(e)
            step(E - 1, more=False)

        @block.tensor
        def _(pe):
            def hidden(e, t):
                c, i, n = t // IT, t % IT, e * TILES + t
                if i == 0:
                    pe.wait_ge(w_in[c % 2], e * (48 * CHUNKS // 2) + (c // 2 * 48 + 48))
                if past(n - 3):
                    pe.wait_ge(s["h"], n - 3)
                for w, cols in ((m["wg"], slice(0, TOK)), (m["wu"], slice(TOK, 2 * TOK))):
                    for k in range(KT):
                        last = nc.tensor.matmul(g["ps"][:, t % 4, cols], w[:, c % 2, k, i * P:(i + 1) * P],
                                                xin[:, k, e].rearrange("p b c -> p (b c)"), start=(k == 0), stop=(k == KT - 1))
                last.then_inc(s["hidden"], 1)

            def down(e, t, n):
                c, i = t // IT, t % IT
                pe.wait_ge(s["h"], n + 1)
                if t == 0 and past(n):
                    pe.wait_ge(s["yfull"], e * NB)
                for b in range(NB):
                    last = nc.tensor.matmul(g["ps"][:, Y + b, :], m["h"][:, t % HRING, b * CAP:(b + 1) * CAP], m["wd"][:, c % 2, i, :],
                                            start=(t == 0), stop=(t == TILES - 1))
                last.then_inc(s["down"], 1)

            def step(e):
                first = isinstance(e, int) and e == 0
                for t in range(TILES):
                    hidden(e, t)
                    if t >= LAG:
                        down(e, t - LAG, e * TILES + (t - LAG))
                    elif not first:
                        down(e - 1, TILES - LAG + t, e * TILES + (t - LAG))

            step(0)
            with pe.Fori(1, E) as e:
                step(e)
            for t in range(TILES - LAG, TILES):
                down(E - 1, t, (E - 1) * TILES + t)

        @block.scalar
        def _(act):
            def step(e):
                for t in range(TILES):
                    n = e * TILES + t
                    act.wait_ge(s["hidden"], n + 1)
                    if past(n - 1):
                        act.wait_ge(s["plus"], n - 1)
                    nc.scalar.activation(m["e"][:, t % 2], g["ps"][:, t % 4, 0:TOK], ACT.Exp, scale=-1.0).then_inc(s["exped"], 1)

            step(0)
            with act.Fori(1, E) as e:
                step(e)

        @block.vector
        def _(dve):
            def outputs(e):
                for b in range(NB):
                    nc.vector.tensor_copy(m["gcol"][:, b:b + 1], gate[:, b].unsqueeze(2)[:, e]).then_inc(s["gcol"], 1)
                dve.wait_ge(s["down"], (e + 1) * TILES)
                dve.wait_ge(s["gcol"], e * NB + NB)
                for b in range(NB):
                    nc.vector.tensor_scalar(m["y"][:, b], g["ps"][:, Y + b, :], m["gcol"][:, b:b + 1], None, ALU.mult).then_inc(s["yfull"], 1)
                for b in range(NB):
                    dve.wait_ge(s["yfull"], e * NB + (b + 1))
                    nc.vector.tensor_copy(y_hi[:, b, e], m["y"][:, b]).then_inc(s["yhi"], 1)
                for b in range(NB):
                    dve.wait_ge(s["yhi"], e * NB + (b + 1))
                    nc.vector.tensor_tensor(y_lo[:, b, e], m["y"][:, b], y_hi[:, b, e].bitcast(F32), ALU.subtract).then_inc(s["ylo"], 1)
                dve.wait_ge(s["ylo"], e * NB + NB)

            def step(e):
                first = isinstance(e, int) and e == 0
                for t in range(TILES):
                    n = e * TILES + t
                    if t == LAG + 1 and not first:
                        outputs(e - 1)
                    dve.wait_ge(s["exped"], n + 1)
                    nc.vector.tensor_scalar(m["r"][:, t % 2], m["e"][:, t % 2], 1.0, None, ALU.add).then_inc(s["plus"], 1)
                    dve.wait_ge(s["plus"], n + 1)
                    nc.vector.reciprocal(m["si"][:, t % 2], m["r"][:, t % 2]).then_inc(s["inv"], 1)
                    dve.wait_ge(s["inv"], n + 1)
                    nc.vector.tensor_tensor(m["r"][:, t % 2], g["ps"][:, t % 4, 0:TOK], m["si"][:, t % 2], ALU.mult).then_inc(s["silu"], 1)
                    dve.wait_ge(s["silu"], n + 1)
                    if past(n + 1 - HRING):
                        dve.wait_ge(s["down"], n + 1 - HRING)
                    nc.vector.tensor_tensor(m["h"][:, t % HRING], g["ps"][:, t % 4, TOK:2 * TOK], m["r"][:, t % 2], ALU.mult).then_inc(s["h"], 1)

            step(0)
            with dve.Fori(1, E) as e:
                step(e)
            outputs(E - 1)


def scatter(nc, g, scat, y_hi, y_lo, out):
    with ExitStack() as ctx:
        s = semaphores(nc, ctx, "sc", "prod sum stored")
        block = ctx.enter_context(nc.Block())

        @block.tensor
        def _(pe):
            for t in range(ROWS):
                b, q = t // QB, t % QB
                for e in range(E):
                    for part in (y_hi, y_lo):
                        last = nc.tensor.matmul(g["ps"][:, t, :], scat[:, b * E + e, q * P:(q + 1) * P], part[:, b, e, :],
                                                start=(e == 0 and part is y_hi), stop=(e == E - 1 and part is y_lo))
                last.then_inc(s["prod"], 1)

        @block.vector
        def _(dve):
            for t in range(ROWS):
                dve.wait_ge(s["prod"], t + 1)
                nc.vector.tensor_tensor(g["x"][:, t, :], g["ps"][:, t, :], g["x"][:, t, :], ALU.add).then_inc(s["sum"], 1)

        @block.sync
        def _(sp):
            for t in range(ROWS):
                sp.wait_ge(s["sum"], t + 1)
                sp.dma_start(out[t * P:(t + 1) * P, :], g["x"][:, t, :]).then_inc(s["stored"], 16)
            sp.wait_ge(s["stored"], 16 * ROWS)


def perceiver_kernel(nc, ins, out):
    scr = {
        "q": nc.dram_tensor("scr_q", [3, NB * D, S], F32).ap(),
        "k": nc.dram_tensor("scr_k", [2, NB * CTX // BANK, D, BANK], F32).ap(),
        "v": nc.dram_tensor("scr_v", [NB * CTX // BANK, XH, P, (BANK // P) * (2 * XD + 1)], F32).ap(),
        "maskbias": nc.dram_tensor("scr_maskbias", [NB, CTX], F32).ap(),
        "sq": nc.dram_tensor("scr_sq", [2, NB, SH * SD, S], F32).ap(),
        "sk": nc.dram_tensor("scr_sk", [2, NB, SH * SD, S], F32).ap(),
    }
    with ExitStack() as whole:
        g = buffers(nc, whole, "all", x=([P, ROWS, D], F32), ident=([P, P], F32), fold=([P, XD + 1], F32))
        g["ps"] = whole.enter_context(nc.psum_tensor("ps", [P, 8, BANK], F32))
        load_residual(nc, g, ins)

        with ExitStack() as ctx:
            m = buffers(nc, ctx, "c0", xT=([P, KT, NB * S], F32))
            normalise_rows(nc, g, "0", m["xT"])
            cross_queries(nc, g, m["xT"], ins, scr)
            project_context(nc, g, ins, scr)
        with ExitStack() as ctx:
            m = buffers(nc, ctx, "c1", o=([P, NB * XH, QB, XD], F32))
            g["o"] = m["o"]
            cross_attention(nc, g, ins, scr)
            output_projection(nc, g, "x", lambda t: m["o"][:, t // QB * XH:(t // QB + 1) * XH, t % QB, :], D,
                              ins["xWo"], ins["xbo"], add=ins["xbv"])
        with ExitStack() as ctx:
            m = buffers(nc, ctx, "s", v=([P, ROWS, SH, SD + 1], F32), o=([P, ROWS, SH, SD], F32), xT=([P, KT, NB * S], F32))
            normalise_rows(nc, g, "1", m["xT"])
            self_projections(nc, g, m["xT"], ins, scr, m["v"][:])
            self_attention(nc, g, ins, scr, m["v"][:], m["o"][:])
            output_projection(nc, g, "s", lambda t: m["o"][:, t].rearrange("p h d -> p (h d)"), SH * SD, ins["sWo"], ins["sbo"])
        with ExitStack() as ctx:
            m = buffers(nc, ctx, "m", scat=([P, NB * E, S], F32R), gate=([P, NB * E], F32), xin=([P, KT, E, NB, CAP], F32))
            with ExitStack() as inner:
                r = buffers(nc, inner, "r", rows=([P, ROWS, D], F32), sel=([P, NB, QB, E * CAP], F32R), xT=([P, KT, NB * S], F32))
                normalise_rows(nc, g, "2", r["xT"], keep=r["rows"])
                route(nc, g, r["xT"], ins, r["sel"], m["scat"], m["gate"])
                gather(nc, g, r["rows"], r["sel"], m["xin"])
            y = buffers(nc, ctx, "y", hi=([P, NB, E, D], F32R), lo=([P, NB, E, D], F32R))
            experts(nc, g, ins, m["xin"], m["gate"][:].rearrange("p (b e) -> p b e", b=NB), y["hi"], y["lo"])
            scatter(nc, g, m["scat"], y["hi"], y["lo"], out)


def laid_out(inputs):
    import numpy as np
    a = {n: np.asarray(v) for n, v in inputs.items()}

    def features(w):
        return w.reshape(-1, P, w.shape[1]).transpose(1, 0, 2)

    fold = np.zeros((P, XD + 1), np.float32)
    fold[:XD, :XD] = fold[XD:2 * XD, :XD] = np.eye(XD)
    fold[2 * XD, XD] = 1.0
    said = {
        "x": a["x"].reshape(NB * S, D),
        "ctx": a["ctx_1024"].reshape(NB * CTX // BANK, BANK, KT, P).transpose(0, 3, 2, 1),
        "mask": a["mask_BxS2_bf1"].view(np.uint8).reshape(NB, CTX),
        "mask_tiles": a["mask_BxS2_bf1"].view(np.uint8).reshape(NB * CTX // BANK, BANK),
        "xWq": features(a["L0_xattn_Wq"].T), "xWk": features(a["L0_xattn_Wk"].T), "xWv": features(a["L0_xattn_Wv"].T),
        "xWo": features(a["L0_xattn_Wo"].T),
        "xbq": a["L0_xattn_bq"].reshape(KT, P).T, "xbk": a["L0_xattn_bk"].reshape(KT, P).T,
        "xbv": a["L0_xattn_bv"], "xbo": a["L0_xattn_bo"],
        "sWq": features(a["L0_attn_Wq"]), "sWk": features(a["L0_attn_Wk"]), "sWv": features(a["L0_attn_Wv"]),
        "sWo": features(a["L0_attn_Wo"]), "sbo": a["L0_attn_bo"],
        "gate_w": features(a["L0_ffn_gate_w"].T),
        "w_gate": a["L0_ffn_w_gate"].reshape(E, INNER // BANK, BANK, KT, P).transpose(0, 1, 4, 3, 2),
        "w_up": a["L0_ffn_w_up"].reshape(E, INNER // BANK, BANK, KT, P).transpose(0, 1, 4, 3, 2),
        "w_down": a["L0_ffn_w_down"].reshape(E, D, INNER // BANK, BANK // P, P).transpose(0, 2, 4, 3, 1),
        "ident": np.eye(P, dtype=np.float32), "fold": fold,
        "tok_row": np.broadcast_to(np.arange(S, dtype=np.float32), (P, S)),
        "tok_col": np.arange(S, dtype=np.float32).reshape(QB, P).T,
    }
    return {n: np.ascontiguousarray(v) for n, v in said.items()}


def kernel(**inputs):
    import numpy as np
    import concourse.bacc as bacc
    from concourse.bass_utils import run_bass_kernel_spmd

    nc = bacc.Bacc("TRN2", target_bir_lowering=False, num_devices=1)
    arrays, args = {}, {}
    for name, a in laid_out(inputs).items():
        arrays[f"in_{name}"] = a
        args[name] = nc.dram_tensor(f"in_{name}", a.shape, mybir.dt.from_np(a.dtype), kind="ExternalInput").ap()
    out = nc.dram_tensor("out", (NB * S, D), F32, kind="ExternalOutput").ap()
    perceiver_kernel(nc, args, out)
    r = run_bass_kernel_spmd(nc, [arrays], core_ids=[0])
    return r.results[0]["out"].reshape(NB, S, D)
```

```python
from contextlib import ExitStack

import concourse.bass as bass
from concourse import mybir
from concourse.alu_op_type import AluOpType as ALU

ACT = mybir.ActivationFunctionType
AX_X = mybir.AxisListType.X
F32 = mybir.dt.float32
F32R = mybir.dt.float32r
U8 = mybir.dt.uint8
U32 = mybir.dt.uint32

P = 128
BANK = 512
NB, S, D = 2, 512, 512
CTX = 8192
KT = D // P
ROWS = NB * S // P
QB = S // P
XH, XD = 16, 32
SH, SD = 16, 64
E, INNER = 8, 2048
CAP = S // E * 2
EPS = 1e-5
MASKED = 1e30


def semaphores(nc, ctx, prefix, names):
    return {n: ctx.enter_context(nc.semaphore(f"{prefix}_{n}")) for n in names.split()}


def semaphores_again(nc, ctx, prefix, names):
    s = {n: nc.alloc_semaphore(f"{prefix}_{n}") for n in names.split()}

    def zero():
        nc.all_engine_barrier()
        nc.clear_and_free_semaphores(list(s.values()))
        nc.all_engine_barrier()

    ctx.callback(zero)
    return s


def buffers(nc, ctx, prefix, **shapes):
    return {n: ctx.enter_context(nc.sbuf_tensor(f"{prefix}_{n}", list(shape), dt)) for n, (shape, dt) in shapes.items()}


def words(ap):
    return ap.bitcast(F32)


def past(value):
    return not isinstance(value, int) or value > 0


def in_groups(engine, size, first, last, step):
    assert (last - first) % size == 0
    with engine.Fori(0, (last - first) // size) as i:
        for u in range(size):
            step(i * size + (first + u), i + (first + u) // size, (first + u) % size)


def in_pairs(engine, first, last, step):
    in_groups(engine, 2, first, last, step)


def fetch(sp, landed, transfers):
    for dst, src in transfers:
        sp.dma_start(dst, src).then_inc(landed, 16)
    return 16 * len(transfers)


def normalise_rows(nc, g, tag, xT=None, split=None, keep=None, first=(), early=()):
    with ExitStack() as ctx:
        s = semaphores(nc, ctx, f"ln{tag}", "landed stats aggr var sd rstd rows turned hi")
        m = buffers(nc, ctx, f"ln{tag}", ve=([P, ROWS], F32),
                    sd=([P, ROWS], F32), rstd=([P, ROWS], F32))
        rows = buffers(nc, ctx, f"ln{tag}", own=([P, ROWS, D], F32))["own"] if keep is None else keep
        block = ctx.enter_context(nc.Block())

        @block.sync
        def _(sp):
            if first:
                fetch(sp, s["landed"], first)
                sp.wait_ge(s["landed"], 16 * len(first))
                if early:
                    fetch(sp, s["landed"], early)
                    sp.wait_ge(s["landed"], 16 * (len(first) + len(early)))

        @block.vector
        def _(dve):
            if first:
                dve.wait_ge(s["landed"], 16 * len(first))
            if first:
                for t in range(ROWS):
                    nc.vector.bn_stats(g["stats"][:, t, :], g["x"][:, t, :]).then_inc(s["stats"], 1)
                for t in range(ROWS):
                    dve.wait_ge(s["stats"], t + 1)
                    nc.vector.bn_aggr(g["moments"][:, t, :], g["stats"][:, t, :]).then_inc(s["aggr"], 1)
                dve.wait_ge(s["aggr"], ROWS)
            nc.vector.tensor_scalar(m["ve"][:], g["moments"][:, :, 1], EPS, None, ALU.add).then_inc(s["var"], 1)
            dve.wait_ge(s["sd"], 1)
            nc.vector.reciprocal(m["rstd"][:], m["sd"][:]).then_inc(s["rstd"], 1)
            dve.wait_ge(s["rstd"], 1)
            for t in range(ROWS):
                nc.vector.tensor_scalar(rows[:, t, :], g["x"][:, t, :], g["moments"][:, t, 0:1], m["rstd"][:, t:t + 1],
                                        ALU.subtract, ALU.mult).then_inc(s["rows"], 1)
            if split is not None:
                for t in range(ROWS):
                    dve.wait_ge(s["hi"], t + 1)
                    nc.vector.tensor_tensor(split[1][:, :, t * P:(t + 1) * P], g["ps"][:, t, :].rearrange("p (k c) -> p k c", k=KT),
                                            split[0][:, :, t * P:(t + 1) * P].bitcast(F32), ALU.subtract)

        @block.tensor
        def _(pe):
            for t in range(ROWS):
                pe.wait_ge(s["rows"], t + 1)
                for k in range(KT):
                    last = nc.tensor.transpose(g["ps"][:, t, k * P:(k + 1) * P], rows[:, t, k * P:(k + 1) * P], g["ident"][:])
                last.then_inc(s["turned"], 1)

        @block.scalar
        def _(act):
            act.wait_ge(s["var"], 1)
            nc.scalar.activation(m["sd"][:], m["ve"][:], ACT.Sqrt).then_inc(s["sd"], 1)
            for t in range(ROWS):
                act.wait_ge(s["turned"], t + 1)
                nc.scalar.copy((xT if split is None else split[0])[:, :, t * P:(t + 1) * P],
                               g["ps"][:, t, :].rearrange("p (k c) -> p k c", k=KT)).then_inc(s["hi"], 1)


def cross_queries(nc, g, xT, ins, scr, w, early):
    with ExitStack() as ctx:
        s = semaphores(nc, ctx, "q", "early mask ones whi wlo bias prod full hi lo stored")
        m = buffers(nc, ctx, "q", full=([P, NB * KT, BANK], F32),
                    hi=([P, NB * KT, BANK], F32R), lo=([P, NB * KT, BANK], F32R),
                    mask=([P, P], U8), bias=([P, P], F32R), ones=([P, CTX // P], F32R))
        block = ctx.enter_context(nc.Block())

        @block.sync
        def _(sp):
            sp.dma_start(m["mask"][:], ins["mask"].rearrange("b (p c) -> (b p) c", c=P)).then_inc(s["mask"], 16)
            waits = fetch(sp, s["early"], early)
            sp.wait_ge(s["ones"], 1)
            sp.dma_start(scr["ones"].rearrange("o (p c) -> (o p) c", p=P), words(m["ones"][:])).then_inc(s["stored"], 16)
            sp.wait_ge(s["bias"], 1)
            sp.dma_start(scr["maskbias"].rearrange("b (p c) -> (b p) c", c=P), words(m["bias"][:])).then_inc(s["stored"], 16)
            for n in range(NB * KT):
                sp.wait_ge(s["lo"], n + 1)
                for i, part in enumerate((m["hi"], m["lo"])):
                    sp.dma_start(scr["q"][i, n * P:(n + 1) * P], words(part[:, n])).then_inc(s["stored"], 16)
            sp.wait_ge(s["early"], waits)
            sp.wait_ge(s["stored"], 16 * (2 + 2 * NB * KT))

        @block.tensor
        def _(pe):
            for n in range(NB * KT):
                b, f = n // KT, n % KT
                for k in range(KT):
                    last = nc.tensor.matmul(g["ps"][:, n, :], w["wq"][:, k, f * P:(f + 1) * P],
                                            xT[:, k, b * S:(b + 1) * S], start=(k == 0), stop=(k == KT - 1))
                last.then_inc(s["prod"], 1)

        @block.vector
        def _(dve):
            nc.vector.memset(words(m["ones"][:]), 1.0).then_inc(s["ones"], 1)
            dve.wait_ge(s["mask"], 16)
            nc.vector.tensor_scalar(m["bias"][:], m["mask"][:], 1.0, MASKED, ALU.subtract, ALU.mult).then_inc(s["bias"], 1)
            for i, (lo, raw, hi) in enumerate(((w["wk_lo"], w["wk"], w["wk_hi"]), (w["wv_lo"], w["wv"], w["wv_hi"]))):
                dve.wait_ge(s["whi"], i + 1)
                nc.vector.tensor_tensor(lo[:], raw[:], hi[:].bitcast(F32), ALU.subtract).then_inc(s["wlo"], 1)
            for n in range(NB * KT):
                dve.wait_ge(s["prod"], n + 1)
                nc.vector.tensor_scalar(m["full"][:, n, :], g["ps"][:, n, :], w["bq"][:, n % KT:n % KT + 1], None,
                                        ALU.add).then_inc(s["full"], 1)
                dve.wait_ge(s["hi"], n + 1)
                nc.vector.tensor_tensor(m["lo"][:, n, :], m["full"][:, n, :], m["hi"][:, n, :].bitcast(F32),
                                        ALU.subtract).then_inc(s["lo"], 1)

        @block.scalar
        def _(act):
            for hi, raw in ((w["wk_hi"], w["wk"]), (w["wv_hi"], w["wv"])):
                nc.scalar.copy(hi[:], raw[:]).then_inc(s["whi"], 1)
            for n in range(NB * KT):
                act.wait_ge(s["full"], n + 1)
                nc.scalar.copy(m["hi"][:, n, :], m["full"][:, n, :]).then_inc(s["hi"], 1)


def project_context(nc, g, ins, scr, w, c):
    TILES = NB * CTX // BANK
    TPB = CTX // BANK
    NC4 = BANK // P
    with ExitStack() as ctx:
        s = semaphores_again(nc, ctx, "proj", "in0 in1 m0 m1 hi lo kprod kfull khi klo vprod vhi vlo ks0 ks1 vs0 vs1")
        raw_in, mask_in = (s["in0"], s["in1"]), (s["m0"], s["m1"])
        k_stored, v_stored = (s["ks0"], s["ks1"]), (s["vs0"], s["vs1"])
        m = buffers(nc, ctx, "proj", kfull=([P, 2, BANK], F32), hi=([P, 2, KT, BANK], F32R), lo=([P, 2, KT, BANK], F32R),
                    khi=([P, 2, KT, BANK], F32R), klo=([P, 2, KT, BANK], F32R),
                    v=([P, 2, XH, NC4, 2 * XD + 1], F32R))
        block = ctx.enter_context(nc.Block())

        @block.sync
        def _(sp):
            def load(j, par):
                sp.dma_start(c["raw"][:, par], ins["ctx"][j]).then_inc(raw_in[par], 16)
                sp.dma_start(c["mask"][:, par], ins["mask_tiles"][j].partition_broadcast(P)).then_inc(mask_in[par], 16)

            def step(j, half, par, more=True):
                sp.wait_ge(s["klo"], j * KT + KT)
                sp.dma_start(scr["k"][0, j].rearrange("(f p) c -> p f c", p=P), words(m["khi"][:, par])).then_inc(k_stored[par], 16)
                sp.dma_start(scr["k"][1, j].rearrange("(f p) c -> p f c", p=P), words(m["klo"][:, par])).then_inc(k_stored[par], 16)
                sp.wait_ge(s["vlo"], j * NC4 + NC4)
                sp.dma_start(scr["v"][j].rearrange("h p c -> p h c"),
                             words(m["v"][:, par].rearrange("p h c e -> p h (c e)"))).then_inc(v_stored[par], 16)
                if more:
                    load(j + 2, par)

            in_pairs(sp, 0, TILES - 2, step)
            step(TILES - 2, TILES // 2 - 1, 0, more=False)
            step(TILES - 1, TILES // 2 - 1, 1, more=False)
            for q in k_stored:
                sp.wait_ge(q, 32 * TILES // 2)
            for q in v_stored:
                sp.wait_ge(q, 16 * TILES // 2)

        @block.tensor
        def _(pe):
            k_passes = ((w["wk_hi"], m["hi"]), (w["wk_hi"], m["lo"]), (w["wk_lo"], m["hi"]))
            v_passes = ((m["hi"], w["wv_hi"]), (m["lo"], w["wv_hi"]), (m["hi"], w["wv_lo"]))

            def step(j, half, par):
                pe.wait_ge(s["lo"], j + 1)
                for f in range(KT):
                    if past(j):
                        pe.wait_ge(s["kfull"], j * KT + (f + 1 - KT))
                    n = 0
                    for weights, tile in k_passes:
                        for k in range(KT):
                            last = nc.tensor.matmul(g["ps"][:, f, :], weights[:, k, f * P:(f + 1) * P], tile[:, par, k, :],
                                                    start=(n == 0), stop=(n == 3 * KT - 1))
                            n += 1
                    last.then_inc(s["kprod"], 1)
                for t in range(NC4):
                    if past(j):
                        pe.wait_ge(s["vlo"], j * NC4 + (t + 1 - NC4))
                    n = 0
                    for tile, weights in v_passes:
                        for k in range(KT):
                            last = nc.tensor.matmul(g["ps"][:, KT + t, :], tile[:, par, k, t * P:(t + 1) * P], weights[:, k, :],
                                                    start=(n == 0), stop=(n == 3 * KT - 1))
                            n += 1
                    last.then_inc(s["vprod"], 1)

            step(0, 0, 0)
            step(1, 0, 1)
            in_pairs(pe, 2, TILES, step)

        def split_hi(act, j, half, par):
            if past(half):
                act.wait_ge(raw_in[par], half * 16)
            if past(j * NC4 - NC4):
                act.wait_ge(s["vprod"], j * NC4 - NC4)
            nc.scalar.copy(m["hi"][:, par].rearrange("p k c -> p (k c)"),
                           c["raw"][:, par].rearrange("p k c -> p (k c)")).then_inc(s["hi"], 1)

        def split_lo(dve, j, par):
            dve.wait_ge(s["hi"], j + 1)
            nc.vector.tensor_tensor(m["lo"][:, par].rearrange("p k c -> p (k c)"),
                                    c["raw"][:, par].rearrange("p k c -> p (k c)"),
                                    m["hi"][:, par].rearrange("p k c -> p (k c)").bitcast(F32),
                                    ALU.subtract).then_inc(s["lo"], 1)

        @block.scalar
        def _(act):
            def step(j, half, par, more=True):
                if past(half):
                    act.wait_ge(k_stored[par], half * 32)
                for f in range(KT):
                    act.wait_ge(s["kfull"], j * KT + (f + 1))
                    nc.scalar.copy(m["khi"][:, par, f, :], m["kfull"][:, f % 2, :]).then_inc(s["khi"], 1)
                if more:
                    split_hi(act, j + 1, half + par, 1 - par)
                if past(half):
                    act.wait_ge(v_stored[par], half * 16)
                for t in range(NC4):
                    act.wait_ge(s["vprod"], j * NC4 + (t + 1))
                    nc.scalar.copy(m["v"][:, par, :, t, 0:XD], g["ps"][:, KT + t, :].rearrange("p (h d) -> p h d", h=XH)
                                   ).then_inc(s["vhi"], 1)

            split_hi(act, 0, 0, 0)
            step(0, 0, 0)
            step(1, 0, 1)
            in_pairs(act, 2, TILES - 2, step)
            step(TILES - 2, TILES // 2 - 1, 0)
            step(TILES - 1, TILES // 2 - 1, 1, more=False)

        @block.vector
        def _(dve):
            def step(j, half, par, more=True):
                if past(half):
                    dve.wait_ge(mask_in[par], half * 16)
                    dve.wait_ge(k_stored[par], half * 32)
                for f in range(KT):
                    dve.wait_ge(s["kprod"], j * KT + (f + 1))
                    if past(j * KT + (f - 1)):
                        dve.wait_ge(s["klo"], j * KT + (f - 1))
                    nc.vector.scalar_tensor_tensor(out=m["kfull"][:, f % 2, :], in0=g["ps"][:, f, :], scalar=w["bk"][:, f:f + 1],
                                                   in1=c["mask"][:, par, :], op0=ALU.add, op1=ALU.mult).then_inc(s["kfull"], 1)
                    dve.wait_ge(s["khi"], j * KT + (f + 1))
                    nc.vector.tensor_tensor(m["klo"][:, par, f, :], m["kfull"][:, f % 2, :],
                                            m["khi"][:, par, f, :].bitcast(F32), ALU.subtract).then_inc(s["klo"], 1)
                if more:
                    split_lo(dve, j + 1, 1 - par)
                if past(half):
                    dve.wait_ge(v_stored[par], half * 16)
                for t in range(NC4):
                    dve.wait_ge(s["vhi"], j * NC4 + (t + 1))
                    nc.vector.tensor_tensor(m["v"][:, par, :, t, XD:2 * XD], g["ps"][:, KT + t, :].rearrange("p (h d) -> p h d", h=XH),
                                            m["v"][:, par, :, t, 0:XD].bitcast(F32), ALU.subtract).then_inc(s["vlo"], 1)

            nc.vector.memset(words(m["v"][:, :, :, :, 2 * XD:]), 1.0)
            split_lo(dve, 0, 0)
            step(0, 0, 0)
            step(1, 0, 1)
            in_pairs(dve, 2, TILES - 2, step)
            step(TILES - 2, TILES // 2 - 1, 0)
            step(TILES - 1, TILES // 2 - 1, 1, more=False)


def cross_attention(nc, g, ins, scr, early):
    HEADS = NB * XH
    NG = CTX // (2 * P)
    RING = 4
    HIGH_LAG = 1
    LOW_LAG = 2
    LAG = 3
    QUARTERS = 4
    KC = CTX // BANK
    TILES = KC * QB
    PER = TILES + 2
    OUT_G = LAG + 2
    ROW_G = NG - 2
    FRESH = NG - 3
    SCALE = float(XD) ** -0.5
    VW = 2 * XD + 1
    ON_VECTOR = [t for t in range(NG - 2) if t % 8 in (0, 3, 6)]
    ON_GPSIMD = [t for t in range(NG) if t not in ON_VECTOR]
    HIGHS = [NG // 8, NG // 2, 7 * NG // 8]
    beside = [2 * ((t - LOW_LAG) % NG in ON_VECTOR) + ((t - HIGH_LAG) % NG in HIGHS) + (t == ROW_G) + (t == LAG) + (t == OUT_G)
              for t in range(NG)]
    chunks, taken, spent = [range(0)] * NG, 0, 0
    for i in range(NG):
        t = (FRESH + i) % NG
        spent += beside[t]
        upto = max(taken, min(TILES, -(-(TILES + sum(beside)) * (i + 1) // NG) - spent))
        chunks[t], taken = range(taken, upto), upto
    assert taken == TILES
    AHEAD = chunks[NG - 1].stop
    k_view = scr["k"].rearrange("s (b q t) (h r) c -> s b q h r t c", b=NB, q=QUARTERS, h=XH)
    v_view = scr["v"].rearrange("(b t) h p c -> b h p t c", b=NB)
    with ExitStack() as ctx:
        s = semaphores_again(nc, ctx, "xa", "early ones k_ones scored p high_dve low_dve low_pool pv ring_in ring_out topped "
                             "maxed row out_read inv q0 q1 m0 m1 v0 v1 " + " ".join(f"k{par}{q}" for par in range(2) for q in range(QUARTERS)))

        def lows(n, t):
            sem, own = (s["low_dve"], ON_VECTOR) if t % NG in ON_VECTOR else (s["low_pool"], ON_GPSIMD)
            return sem, (n + t // NG) * len(own) + (own.index(t % NG) + 1)

        def highs(n, t):
            return (n + t // NG) * len(HIGHS) + (HIGHS.index(t % NG) + 1)

        q_in, qmax_in, v_in = (s["q0"], s["q1"]), (s["m0"], s["m1"]), (s["v0"], s["v1"])
        k_in = ((s["k00"], s["k01"], s["k02"], s["k03"]), (s["k10"], s["k11"], s["k12"], s["k13"]))
        m = buffers(nc, ctx, "xa", k=([P, 2, CTX], F32R), v=([P, 2, CTX // P, VW], F32R),
                    q=([P, 2, S], F32R), qmax=([P, 2, S], F32R),
                    full=([P, RING, 2 * BANK], F32), hi=([P, RING, 2 * BANK], F32R), lo=([P, RING, 2 * BANK], F32R),
                    mx=([P, QB, KC], F32), top=([P, QB], F32), row=([P, QB, 2], F32), o=([P, S], F32), den=([P, QB], F32))
        O, R, BANKS = 4, 5, 3
        block = ctx.enter_context(nc.Block())

        @block.sync
        def _(sp):
            def load_k(b, h, par, q):
                cols = slice(q * CTX // QUARTERS, (q + 1) * CTX // QUARTERS)
                for part, row in ((0, 0), (1, XD), (0, 2 * XD)):
                    sp.dma_start(words(m["k"][row:row + XD, par, cols].rearrange("r (t c) -> r t c", c=BANK)),
                                 k_view[part, b, q, h]).then_inc(k_in[par][q], 16)
                sp.dma_start(words(m["k"][3 * XD:3 * XD + 1, par, cols]),
                             scr["maskbias"][b:b + 1, cols] if isinstance(b, int) else scr["maskbias"][bass.ds(b, 1), cols]
                             ).then_inc(k_in[par][q], 16)

            def load_q(n, par, dst, sem):
                for part, row in ((0, 0), (0, XD), (1, 2 * XD)):
                    sp.dma_start(words(dst[row:row + XD, par, :]),
                                 scr["q"][part].rearrange("(n r) c -> n r c", r=XD)[n]).then_inc(sem[par], 16)

            def load_v(b, h, par):
                sp.dma_start(words(m["v"][:, par].rearrange("p (t c) e -> p t (c e)", c=BANK // P)), v_view[b, h]).then_inc(v_in[par], 16)

            def step(n, half, par, more=True):
                if past(n):
                    sp.wait_ge(s["scored"], n * NG)
                load_k((n + 1) // XH, (n + 1) % XH, 1 - par, QUARTERS - 1)
                load_q(n + 1, 1 - par, m["q"], q_in)
                if more:
                    sp.wait_ge(s["ring_in"], n * PER + TILES)
                    load_q(n + 2, par, m["qmax"], qmax_in)
                if past(n):
                    sp.wait_ge(s["pv"], n * NG)
                load_v((n + 1) // XH, (n + 1) % XH, 1 - par)
                if more:
                    for q in range(QUARTERS - 1):
                        sp.wait_ge(s["scored"], n * NG + (q + 1) * (NG // QUARTERS))
                        load_k((n + 2) // XH, (n + 2) % XH, par, q)

            load_q(0, 0, m["qmax"], qmax_in)
            for q in range(QUARTERS):
                load_k(0, 0, 0, q)
            load_q(0, 0, m["q"], q_in)
            for par in range(2):
                sp.dma_start(words(m["k"][3 * XD + 1:3 * XD + 2, par]), scr["ones"]).then_inc(s["k_ones"], 16)
            load_v(0, 0, 0)
            load_q(1, 1, m["qmax"], qmax_in)
            for q in range(QUARTERS - 1):
                load_k(0, 1, 1, q)
            step(0, 0, 0)
            step(1, 0, 1)
            in_pairs(sp, 2, HEADS - 2, step)
            step(HEADS - 2, HEADS // 2 - 1, 0, more=False)
            sp.wait_ge(s["early"], fetch(sp, s["early"], early))

        def ring_base(n):
            if isinstance(n, int) and n == HEADS - 1:
                return n * PER + TILES
            return n * PER + TILES + AHEAD if not isinstance(n, int) or n > 0 else TILES + 1 + AHEAD

        def ring_slots(n):
            assert PER % BANKS == 0
            return (ring_base(n) if isinstance(n, int) else TILES + AHEAD) % BANKS

        @block.tensor
        def _(pe):
            def ring_slot(entry, slot):
                if past(entry + 1 - BANKS):
                    pe.wait_ge(s["ring_out"], entry + 1 - BANKS)
                return g["ps"][:, R + slot, :]

            def max_product(half, par, idx, entry, slot):
                kc, qb = idx // QB, idx % QB
                if idx == 0:
                    pe.wait_ge(qmax_in[par], half * 48 + 48)
                if qb == 0 and kc % (KC // QUARTERS) == 0:
                    pe.wait_ge(k_in[par][kc // (KC // QUARTERS)], half * 64 + 64)
                out = ring_slot(entry, slot)
                nc.tensor.matmul(out, m["qmax"][0:3 * XD + 1, par, qb * P:(qb + 1) * P],
                                 m["k"][0:3 * XD + 1, par, kc * BANK:(kc + 1) * BANK], start=True, stop=True
                                 ).then_inc(s["ring_in"], 1)

            def turn_maxima(n, entry, slot):
                pe.wait_ge(s["maxed"], n + 1)
                out = ring_slot(entry, slot)
                for qb in range(QB):
                    last = nc.tensor.matmul(out[3 * XD:3 * XD + 2, qb * P:(qb + 1) * P], m["row"][:, qb, :], g["ident"][:],
                                            start=True, stop=True)
                last.then_inc(s["ring_in"], 1)

            def turn_output(n, entry, slot):
                pe.wait_ge(s["out_read"], n + 2)
                out = ring_slot(entry, slot)
                for qb in range(QB):
                    last = nc.tensor.matmul(out[:, qb * P:qb * P + XD + 1], m["o"][0:VW, qb * P:(qb + 1) * P], g["fold"][0:VW, :],
                                            start=True, stop=True)
                last.then_inc(s["ring_in"], 1)

            def values(n, half, par, t, c):
                if t == 0 and c == 0:
                    pe.wait_ge(v_in[par], half * 16 + 16)
                    pe.wait_ge(s["out_read"], n + 1)
                if c == 0:
                    pe.wait_ge(*lows(n, t))
                for part in (m["hi"], m["lo"]):
                    last = nc.tensor.matmul(g["ps"][0:VW, O, :], m["v"][:, par, 2 * t + c, :],
                                            part[:, t % RING, c * BANK:(c + 1) * BANK],
                                            start=(t == 0 and c == 0 and part is m["hi"]),
                                            stop=(t == NG - 1 and c == 1 and part is m["lo"]))
                if c == 1:
                    last.then_inc(s["pv"], 1)

            def step(n, half, par, maxima=True, ahead=True):
                entry, r = ring_base(n), ring_slots(n)
                first = isinstance(n, int) and n == 0
                for t in range(NG):
                    group = n * NG + t
                    if t == 0:
                        pe.wait_ge(q_in[par], half * 48 + 48)
                        pe.wait_ge(s["row"], n + 1)
                    if past(group - 1):
                        pe.wait_ge(s["p"], group - 1)
                    for c in range(2):
                        key = (2 * t + c) * P
                        last = nc.tensor.matmul(g["ps"][:, 2 * (t % 2) + c, :], m["k"][0:3 * XD + 2, par, key:key + P],
                                                m["q"][0:3 * XD + 2, par, :], start=True, stop=True)
                    last.then_inc(s["scored"], 1)
                    todo = list(chunks[t]) if (maxima if t < FRESH else ahead) else []
                    for c in range(2):
                        for idx in todo[:2] if c == 0 else todo[2:]:
                            max_product(*((half + par, 1 - par) if t < FRESH else (half + 1, par)), idx, entry, r % BANKS)
                            entry, r = entry + 1, r + 1
                        if t >= LAG:
                            values(n, half, par, t - LAG, c)
                        elif not first:
                            values(n - 1, half + par - 1, 1 - par, NG - LAG + t, c)
                    if t == ROW_G and maxima:
                        turn_maxima(n + 1, entry, r % BANKS)
                        entry, r = entry + 1, r + 1
                    if t == OUT_G and not first:
                        turn_output(n - 1, entry, r % BANKS)
                        entry, r = entry + 1, r + 1

            pe.wait_ge(s["ones"], 1)
            for idx in range(TILES):
                max_product(0, 0, idx, idx, idx % BANKS)
            pe.wait_ge(s["k_ones"], 32)
            turn_maxima(0, TILES, TILES % BANKS)
            for idx in range(AHEAD):
                max_product(0, 1, idx, TILES + 1 + idx, (TILES + 1 + idx) % BANKS)
            step(0, 0, 0)
            in_pairs(pe, 1, HEADS - 3, step)
            step(HEADS - 3, HEADS // 2 - 2, 1)
            step(HEADS - 2, HEADS // 2 - 1, 0, ahead=False)
            n = HEADS - 1
            step(n, n // 2, n % 2, maxima=False, ahead=False)
            for t in range(NG - LAG, NG):
                for c in range(2):
                    values(n, n // 2, n % 2, t, c)
            turn_output(n, ring_base(n) + 1, (ring_base(n) + 1) % BANKS)

        @block.scalar
        def _(act):
            def step(n, half, par):
                for t in range(NG):
                    group = n * NG + t
                    act.wait_ge(s["scored"], group + 1)
                    if past(group + 1 - RING):
                        act.wait_ge(*lows(n, t - RING))
                    scores = g["ps"][:, 2 * (t % 2):2 * (t % 2) + 2, :].rearrange("p a c -> p (a c)")
                    last = nc.scalar.activation(m["full"][:, t % RING, :], scores, ACT.Exp, scale=SCALE)
                    if t not in HIGHS:
                        if past(group + 1 - RING):
                            act.wait_ge(s["pv"], group + 1 - RING)
                        last = nc.scalar.activation(m["hi"][:, t % RING, :], scores, ACT.Exp, scale=SCALE)
                    last.then_inc(s["p"], 1)

            step(0, 0, 0)
            in_pairs(act, 1, HEADS - 1, step)
            step(HEADS - 1, HEADS // 2 - 1, 1)

        @block.gpsimd
        def _(pool):
            def step(n, half, par):
                for t in ON_GPSIMD:
                    group = n * NG + t
                    pool.wait_ge(s["p"], group + 1)
                    if t in HIGHS:
                        pool.wait_ge(s["high_dve"], highs(n, t))
                    if past(group + 1 - RING):
                        pool.wait_ge(s["pv"], group + 1 - RING)
                    nc.gpsimd.tensor_tensor(m["lo"][:, t % RING, :], m["full"][:, t % RING, :],
                                            m["hi"][:, t % RING, :].bitcast(F32), ALU.subtract).then_inc(s["low_pool"], 1)

            step(0, 0, 0)
            in_pairs(pool, 1, HEADS - 1, step)
            step(HEADS - 1, HEADS // 2 - 1, 1)

        @block.vector
        def _(dve):
            def read_max(idx, entry, slot):
                dve.wait_ge(s["ring_in"], entry + 1)
                kc, qb = idx // QB, idx % QB
                nc.vector.tensor_reduce(m["mx"][:, qb, kc:kc + 1], g["ps"][:, R + slot, :], AX_X, ALU.max
                                        ).then_inc(s["ring_out"], 1)

            def finish_maxima(n, entry):
                dve.wait_ge(s["ring_out"], entry)
                nc.vector.tensor_reduce(m["top"][:], m["mx"][:], AX_X, ALU.max).then_inc(s["topped"], 1)
                dve.wait_ge(s["topped"], n + 1)
                nc.vector.tensor_scalar(m["row"][:, :, 1], m["top"][:], -1.0, None, ALU.mult).then_inc(s["maxed"], 1)

            def read_row(n, half, par, entry, slot):
                dve.wait_ge(s["ring_in"], entry + 1)
                if past(n - 1):
                    dve.wait_ge(s["scored"], (n - 1) * NG)
                nc.vector.tensor_copy(m["q"][3 * XD:3 * XD + 2, par, :], g["ps"][3 * XD:3 * XD + 2, R + slot, :]
                                      ).then_inc(s["row"], 1)
                dve.wait_ge(s["row"], n + 1)
                dve.sem_inc(s["ring_out"], 1)

            def read_output(n):
                dve.wait_ge(s["pv"], (n + 1) * NG)
                nc.vector.tensor_copy(m["o"][0:VW, :], g["ps"][0:VW, O, :]).then_inc(s["out_read"], 1)

            def write_output(n, entry, slot):
                dve.wait_ge(s["ring_in"], entry + 1)
                out = g["ps"][:, R + slot, :].rearrange("p (q c) -> p q c", q=QB)
                nc.vector.reciprocal(m["den"][:], out[:, :, XD]).then_inc(s["inv"], 1)
                dve.wait_ge(s["inv"], n + 1)
                nc.vector.tensor_tensor(g["o"][:, n], out[:, :, 0:XD],
                                        m["den"][:].unsqueeze(2).to_broadcast([P, QB, XD]), ALU.mult).then_inc(s["ring_out"], 1)

            def high_part(t, group):
                dve.wait_ge(s["p"], group + 1)
                if past(group + 1 - RING):
                    dve.wait_ge(s["pv"], group + 1 - RING)
                nc.vector.tensor_copy(m["hi"][:, t % RING, :], m["full"][:, t % RING, :]).then_inc(s["high_dve"], 1)

            def low_part(n, t, group):
                dve.wait_ge(s["p"], group + 1)
                if t in HIGHS:
                    dve.wait_ge(s["high_dve"], highs(n, t))
                if past(group + 1 - RING):
                    dve.wait_ge(s["pv"], group + 1 - RING)
                nc.vector.tensor_tensor(m["lo"][:, t % RING, :], m["full"][:, t % RING, :],
                                        m["hi"][:, t % RING, :].bitcast(F32), ALU.subtract).then_inc(s["low_dve"], 1)

            def step(n, half, par, maxima=True, ahead=True):
                entry, r = ring_base(n), ring_slots(n)
                first = isinstance(n, int) and n == 0
                for t in range(NG):
                    if t == LAG and not first:
                        read_output(n - 1)
                    at = t - HIGH_LAG
                    if at % NG in HIGHS and (at >= 0 or not first):
                        high_part(at % NG, n * NG + at)
                    at = t - LOW_LAG
                    if at % NG in ON_VECTOR and (at >= 0 or not first):
                        low_part(n if at >= 0 else n - 1, at % NG, n * NG + at)
                    for idx in chunks[t] if (maxima if t < FRESH else ahead) else ():
                        read_max(idx, entry, r % BANKS)
                        entry, r = entry + 1, r + 1
                        if idx == TILES - 1:
                            finish_maxima(n + 1, entry)
                    if t == ROW_G and maxima:
                        read_row(n + 1, half + par, 1 - par, entry, r % BANKS)
                        entry, r = entry + 1, r + 1
                    if t == OUT_G and not first:
                        write_output(n - 1, entry, r % BANKS)
                        entry, r = entry + 1, r + 1

            dve.sem_inc(s["out_read"], 1)
            nc.vector.memset(m["row"][:], 1.0)
            nc.vector.memset(words(m["q"][3 * XD:3 * XD + 2]), 1.0)
            nc.vector.memset(words(m["qmax"][3 * XD:3 * XD + 2]), 1.0).then_inc(s["ones"], 1)
            dve.wait_ge(s["ones"], 1)
            for idx in range(TILES):
                read_max(idx, idx, idx % BANKS)
            finish_maxima(0, TILES)
            read_row(0, 0, 0, TILES, TILES % BANKS)
            for idx in range(AHEAD):
                read_max(idx, TILES + 1 + idx, (TILES + 1 + idx) % BANKS)
            step(0, 0, 0)
            in_pairs(dve, 1, HEADS - 3, step)
            step(HEADS - 3, HEADS // 2 - 2, 1)
            step(HEADS - 2, HEADS // 2 - 1, 0, ahead=False)
            n = HEADS - 1
            step(n, n // 2, n % 2, maxima=False, ahead=False)
            for t in range(NG - LOW_LAG, NG):
                if t in HIGHS and t + HIGH_LAG >= NG:
                    high_part(t, n * NG + t)
                if t in ON_VECTOR:
                    low_part(n, t, n * NG + t)
            read_output(n)
            write_output(n, ring_base(n) + 1, (ring_base(n) + 1) % BANKS)


def output_projection(nc, g, tag, rows, width, w, bias, add=None, split=None, load=None):
    KW = width // P
    HALVES = -(-KW // 4)
    with ExitStack() as ctx:
        s = semaphores(nc, ctx, f"out{tag}", "landed rows whi wlo turned hi lo prod added done stats split_hi")
        m = buffers(nc, ctx, f"out{tag}", w_hi=([P, KW, D], F32R), w_lo=([P, KW, D], F32R),
                    **({} if add is None else {"rows": ([P, 2, width], F32)}), hi=([P, 2, KW * P], F32R), lo=([P, 2, KW * P], F32R))
        T, Y = 0, 4
        block = ctx.enter_context(nc.Block())

        if split is not None:
            @block.sync
            def _(sp):
                sp.dma_start(split[2][:], load).then_inc(s["landed"], 16)

        def turned(t, half):
            return g["ps"][:, T + 2 * (t % 2) + half, :]

        @block.vector
        def _(dve):
            def take_rows(t):
                if t >= 2:
                    dve.wait_ge(s["turned"], t - 1)
                nc.vector.tensor_tensor(m["rows"][:, t % 2, :].rearrange("p (h d) -> p h d", d=XD), rows(t),
                                        add[:].rearrange("p (h d) -> p h d", d=XD), ALU.add).then_inc(s["rows"], 1)

            def low(t):
                dve.wait_ge(s["hi"], t + 1)
                if t >= 2:
                    dve.wait_ge(s["prod"], t - 1)
                for half in range(HALVES):
                    at = slice(half * BANK, (half + 1) * BANK)
                    last = nc.vector.tensor_tensor(m["lo"][:, t % 2, at], turned(t, half),
                                                   m["hi"][:, t % 2, at].bitcast(F32), ALU.subtract)
                last.then_inc(s["lo"], 1)

            def accumulate(t):
                dve.wait_ge(s["prod"], t + 1)
                nc.vector.tensor_tensor(g["x"][:, t, :], g["ps"][:, Y + t % 2, :], g["x"][:, t, :], ALU.add).then_inc(s["added"], 1)
                dve.wait_ge(s["added"], t + 1)
                nc.vector.tensor_tensor(g["x"][:, t, :], g["x"][:, t, :], bias[:], ALU.add).then_inc(s["done"], 1)
                if t > 0:
                    moments(t - 1)

            def moments(t):
                dve.wait_ge(s["done"], t + 1)
                nc.vector.bn_stats(g["stats"][:, t, :], g["x"][:, t, :]).then_inc(s["stats"], 1)
                dve.wait_ge(s["stats"], t + 1)
                nc.vector.bn_aggr(g["moments"][:, t, :], g["stats"][:, t, :])

            if add is not None:
                take_rows(0)
                take_rows(1)
            for k in range(KW):
                dve.wait_ge(s["whi"], k + 1)
                nc.vector.tensor_tensor(m["w_lo"][:, k], w[:, k], m["w_hi"][:, k].bitcast(F32), ALU.subtract).then_inc(s["wlo"], 1)
            low(0)
            for t in range(ROWS):
                if t + 1 < ROWS:
                    low(t + 1)
                if t + 2 < ROWS and add is not None:
                    take_rows(t + 2)
                if split is not None and t < KT:
                    dve.wait_ge(s["split_hi"], t + 1)
                    nc.vector.tensor_tensor(split[1][:, t], split[2][:, t], split[0][:, t].bitcast(F32), ALU.subtract)
                accumulate(t)
            moments(ROWS - 1)

        @block.scalar
        def _(act):
            def high(t):
                act.wait_ge(s["turned"], t + 1)
                if t >= 2:
                    act.wait_ge(s["prod"], t - 1)
                for half in range(HALVES):
                    last = nc.scalar.copy(m["hi"][:, t % 2, half * BANK:(half + 1) * BANK], turned(t, half))
                last.then_inc(s["hi"], 1)

            for k in range(KW):
                nc.scalar.copy(m["w_hi"][:, k], w[:, k]).then_inc(s["whi"], 1)
            high(0)
            for t in range(ROWS):
                if t + 1 < ROWS:
                    high(t + 1)
                if split is not None and t < KT:
                    act.wait_ge(s["landed"], 16)
                    nc.scalar.copy(split[0][:, t], split[2][:, t]).then_inc(s["split_hi"], 1)

        @block.tensor
        def _(pe):
            def turn(t):
                if add is not None:
                    pe.wait_ge(s["rows"], t + 1)
                if t >= 2:
                    pe.wait_ge(s["lo"], t - 1)
                for k in range(KW):
                    last = nc.tensor.transpose(turned(t, k // 4)[:, k % 4 * P:(k % 4 + 1) * P],
                                               (rows(t) if add is None else m["rows"][:, t % 2])[:, k * P:(k + 1) * P], g["ident"][:])
                last.then_inc(s["turned"], 1)

            turn(0)
            for t in range(ROWS):
                if t + 1 < ROWS:
                    turn(t + 1)
                pe.wait_ge(s["lo"], t + 1)
                if t >= 2:
                    pe.wait_ge(s["added"], t - 1)
                if t == 0:
                    pe.wait_ge(s["wlo"], KW)
                count = 0
                for part, weights in ((m["hi"], m["w_hi"]), (m["lo"], m["w_hi"]), (m["hi"], m["w_lo"])):
                    for k in range(KW):
                        last = nc.tensor.matmul(g["ps"][:, Y + t % 2, :], part[:, t % 2, k * P:(k + 1) * P], weights[:, k, :],
                                                start=(count == 0), stop=(count == 3 * KW - 1))
                        count += 1
                last.then_inc(s["prod"], 1)


def self_projections(nc, g, x_hi, x_lo, ins, scr, v, w, w_hi, w_lo):
    FT = SH * SD // P
    OUTS = NB * FT
    VOUT = ROWS * SH * SD // BANK
    SLOTS = 4
    BANKS = 8
    with ExitStack() as ctx:
        s = semaphores(nc, ctx, "sp", "w whi wlo prod hi lo vread st0 st1 st2 st3")
        stored = (s["st0"], s["st1"], s["st2"], s["st3"])
        m = buffers(nc, ctx, "sp", hi=([P, SLOTS, BANK], F32R), lo=([P, SLOTS, BANK], F32R))
        block = ctx.enter_context(nc.Block())

        @block.sync
        def _(sp):
            for i in range(2):
                if i:
                    sp.wait_ge(s["wlo"], KT)
                sp.dma_start(w[:], (ins["sWk"], ins["sWv"])[i]).then_inc(s["w"], 16)
                dst = (scr["sq"], scr["sk"])[i]
                for n in range(OUTS):
                    o = i * OUTS + n
                    rows = slice(n % FT * P, (n % FT + 1) * P)
                    sp.wait_ge(s["lo"], o + 1)
                    sp.dma_start(dst[0, n // FT, rows], words(m["hi"][:, o % SLOTS])).then_inc(stored[o % SLOTS], 16)
                    sp.dma_start(dst[1, n // FT, rows], words(m["lo"][:, o % SLOTS])).then_inc(stored[o % SLOTS], 16)
            for q in stored:
                sp.wait_ge(q, 32 * 2 * OUTS // SLOTS)

        @block.tensor
        def _(pe):
            for o in range(2 * OUTS + VOUT):
                i, n = (o // OUTS, o % OUTS) if o < 2 * OUTS else (2, o - 2 * OUTS)
                if n == 0 and i:
                    pe.wait_ge(s["wlo"], i * KT)
                if o >= BANKS:
                    if o - BANKS < 2 * OUTS:
                        pe.wait_ge(s["lo"], o - BANKS + 1)
                    else:
                        pe.wait_ge(s["vread"], o - BANKS - 2 * OUTS + 1)
                count = 0
                for x, weights in ((x_hi, w_hi), (x_lo, w_hi), (x_hi, w_lo)):
                    for k in range(KT):
                        wk = weights[:, i % 2, k]
                        if i < 2:
                            lhsT, rhs = wk[:, n % FT * P:(n % FT + 1) * P], x[:, k, n // FT * S:(n // FT + 1) * S]
                        else:
                            lhsT, rhs = x[:, k, n // 2 * P:(n // 2 + 1) * P], wk[:, n % 2 * BANK:(n % 2 + 1) * BANK]
                        last = nc.tensor.matmul(g["ps"][:, o % BANKS, :], lhsT, rhs, start=(count == 0), stop=(count == 3 * KT - 1))
                        count += 1
                last.then_inc(s["prod"], 1)

        PIECES = {4 + 2 * k: k for k in range(KT)}

        @block.scalar
        def _(act):
            for o in range(2 * OUTS):
                i = o // OUTS
                if o % OUTS in PIECES:
                    k = PIECES[o % OUTS]
                    act.wait_ge(s["w"], 16 * i + 16)
                    nc.scalar.copy(w_hi[:, 1 - i, k], w[:, k]).then_inc(s["whi"], 1)
                act.wait_ge(s["prod"], o + 1)
                if o >= SLOTS:
                    act.wait_ge(stored[o % SLOTS], 32 * (o // SLOTS))
                nc.scalar.copy(m["hi"][:, o % SLOTS], g["ps"][:, o % BANKS, :]).then_inc(s["hi"], 1)

        @block.vector
        def _(dve):
            nc.vector.memset(v[:, :, :, SD:], 1.0)
            for o in range(2 * OUTS):
                i = o // OUTS
                if o % OUTS in PIECES:
                    k = PIECES[o % OUTS]
                    dve.wait_ge(s["whi"], i * KT + k + 1)
                    nc.vector.tensor_tensor(w_lo[:, 1 - i, k], w[:, k], w_hi[:, 1 - i, k].bitcast(F32),
                                            ALU.subtract).then_inc(s["wlo"], 1)
                dve.wait_ge(s["hi"], o + 1)
                nc.vector.tensor_tensor(m["lo"][:, o % SLOTS], g["ps"][:, o % BANKS, :], m["hi"][:, o % SLOTS].bitcast(F32),
                                        ALU.subtract).then_inc(s["lo"], 1)
            for n in range(VOUT):
                dve.wait_ge(s["prod"], 2 * OUTS + n + 1)
                nc.vector.tensor_copy(v[:, n // 2, n % 2 * (SH // 2):(n % 2 + 1) * (SH // 2), 0:SD],
                                      g["ps"][:, (2 * OUTS + n) % BANKS, :].rearrange("p (h d) -> p h d", d=SD)
                                      ).then_inc(s["vread"], 1)


def self_attention(nc, g, ins, scr, v, out, early):
    HEADS = NB * SH
    NG = S // (2 * P)
    BUFS = 4
    BANKS = 3
    VW = SD + 1
    SCALE = float(SD) ** -0.5
    PER = QB + 2
    with ExitStack() as ctx:
        s = semaphores(nc, ctx, "sa", "early ones head_v scored p low_dve low_pool pv ring_in ring_out maxed row out_read inv in0 in1 in2 in3")
        landed = (s["in0"], s["in1"], s["in2"], s["in3"])
        m = buffers(nc, ctx, "sa", q1=([P, BUFS, S], F32R), q2=([P, BUFS, S], F32R), k1=([P, BUFS, S], F32R), k2=([P, BUFS, S], F32R),
                    v=([P, BUFS, QB, VW], F32), v_hi=([P, BUFS, QB, VW], F32R), v_lo=([P, BUFS, QB, VW], F32R),
                    full=([P, 2, 2 * BANK], F32), hi=([P, 2 * NG, 2 * BANK], F32R), lo=([P, 2 * NG, 2 * BANK], F32R), mx=([P, QB], F32), row=([P, QB], F32),
                    o=([P, S], F32), den=([P, QB], F32))
        O, R = 4, 5
        block = ctx.enter_context(nc.Block())

        @block.sync
        def _(sp):
            def load(n, buf):
                q, k = (t.rearrange("s b (h r) c -> s b h r c", h=SH) for t in (scr["sq"], scr["sk"]))
                b, h = n // SH, n % SH
                for dst, row, src in ((m["q1"], 0, q[0]), (m["q1"], SD, q[0]), (m["q2"], 0, q[1]),
                                      (m["k1"], 0, k[0]), (m["k1"], SD, k[1]), (m["k2"], 0, k[0])):
                    sp.dma_start(words(dst[row:row + SD, buf]), src[b, h]).then_inc(landed[buf], 16)

            def step(n, turn, buf):
                if past(n):
                    sp.wait_ge(s["scored"], n * NG)
                load(n + 3, (buf + 3) % BUFS)

            sp.wait_ge(s["ones"], 1)
            for n in range(3):
                load(n, n)
            step(0, 0, 0)
            in_groups(sp, 4, 1, HEADS - 3, step)
            sp.wait_ge(s["early"], fetch(sp, s["early"], early))

        @block.gpsimd
        def _(pool):
            v_of = v.rearrange("p (b q) h c -> p b h q c", b=NB)

            def low_part(n, par):
                pool.wait_ge(s["p"], n * NG + 2)
                if past(n - 1):
                    pool.wait_ge(s["pv"], (n - 1) * NG)
                nc.gpsimd.tensor_tensor(m["lo"][:, par * NG + 1, :], m["full"][:, 1, :],
                                        m["hi"][:, par * NG + 1, :].bitcast(F32), ALU.subtract).then_inc(s["low_pool"], 1)

            def split_values(n, buf):
                if past(n - 3):
                    pool.wait_ge(s["pv"], (n - 3) * NG)
                nc.gpsimd.tensor_copy(m["v"][:, buf], v_of[:, n // SH, n % SH]).then_inc(s["head_v"], 1)
                nc.gpsimd.tensor_copy(m["v_hi"][:, buf], v_of[:, n // SH, n % SH]).then_inc(s["head_v"], 1)
                pool.wait_ge(s["head_v"], n * 3 + 2)
                nc.gpsimd.tensor_tensor(m["v_lo"][:, buf], m["v"][:, buf], m["v_hi"][:, buf].bitcast(F32),
                                        ALU.subtract).then_inc(s["head_v"], 1)

            def step(n, turn, buf):
                low_part(n - 3, (buf + 1) % 2)
                split_values(n, buf)

            for n in range(4):
                split_values(n, n)
            low_part(0, 0)
            in_groups(pool, 4, 4, HEADS, step)
            for n in range(HEADS - 3, HEADS):
                low_part(n, n % 2)

        def ring_base(n):
            return n * PER + 3 if not isinstance(n, int) or n >= 2 else (n + 1) * (PER - 1)

        def ring_slots(n):
            assert PER % BANKS == 0
            return (ring_base(n) if isinstance(n, int) else 3) % BANKS

        @block.tensor
        def _(pe):
            def ring_slot(entry, slot):
                if past(entry + 1 - BANKS):
                    pe.wait_ge(s["ring_out"], entry + 1 - BANKS)
                return g["ps"][:, R + slot, :]

            def max_product(turn, buf, qb, entry, slot):
                if qb == 0:
                    pe.wait_ge(landed[buf], turn * 96 + 96)
                nc.tensor.matmul(ring_slot(entry, slot), m["q1"][:, buf, qb * P:(qb + 1) * P], m["k1"][:, buf, :],
                                 start=True, stop=True).then_inc(s["ring_in"], 1)

            def turn_maxima(n, entry, slot):
                pe.wait_ge(s["maxed"], n + 1)
                out = ring_slot(entry, slot)
                for qb in range(QB):
                    last = nc.tensor.matmul(out[SD:SD + 1, qb * P:(qb + 1) * P], m["row"][:, qb:qb + 1], g["ident"][:],
                                            start=True, stop=True)
                last.then_inc(s["ring_in"], 1)

            def turn_output(n, entry, slot):
                pe.wait_ge(s["out_read"], n + 2)
                out = ring_slot(entry, slot)
                for qb in range(QB):
                    last = nc.tensor.matmul(out[:, qb * P:qb * P + VW], m["o"][0:VW, qb * P:(qb + 1) * P], g["ident"][0:VW, 0:VW],
                                            start=True, stop=True)
                last.then_inc(s["ring_in"], 1)

            def values(n, buf, t):
                if t == 0:
                    pe.wait_ge(s["head_v"], n * 3 + 3)
                    pe.wait_ge(s["out_read"], n + 1)
                pe.wait_ge(s["low_pool" if t else "low_dve"], n + 1)
                slot = buf % 2 * NG + t
                for c in range(2):
                    for i, (part, vp) in enumerate(((m["hi"], m["v_hi"]), (m["hi"], m["v_lo"]), (m["lo"], m["v_hi"]))):
                        last = nc.tensor.matmul(g["ps"][0:VW, O, :], vp[:, buf, 2 * t + c, :],
                                                part[:, slot, c * BANK:(c + 1) * BANK],
                                                start=(t == 0 and c == 0 and i == 0), stop=(t == NG - 1 and c == 1 and i == 2))
                last.then_inc(s["pv"], 1)

            def scores(n, buf, t):
                if t == 0:
                    pe.wait_ge(s["row"], n + 1)
                if past(n * NG + (t - 1)):
                    pe.wait_ge(s["p"], n * NG + (t - 1))
                for c in range(2):
                    key = slice((2 * t + c) * P, (2 * t + c + 1) * P)
                    nc.tensor.matmul(g["ps"][:, 2 * t + c, :], m["k1"][:, buf, key], m["q1"][:, buf, :], start=True, stop=False)
                    last = nc.tensor.matmul(g["ps"][:, 2 * t + c, :], m["k2"][0:SD + 1, buf, key], m["q2"][0:SD + 1, buf, :],
                                            start=False, stop=True)
                last.then_inc(s["scored"], 1)

            def step(n, turn, buf, maxima=True):
                entry, r = ring_base(n), ring_slots(n)
                known = n if isinstance(n, int) else 2
                nturn, nbuf = turn + (buf + 1) // BUFS, (buf + 1) % BUFS
                scores(n, buf, 0)
                if maxima:
                    for qb in range(QB - 1):
                        max_product(nturn, nbuf, qb, entry, r % BANKS)
                        entry, r = entry + 1, r + 1
                if known >= 1:
                    values(n - 1, (buf - 1) % BUFS, 0)
                if maxima:
                    max_product(nturn, nbuf, QB - 1, entry, r % BANKS)
                    entry, r = entry + 1, r + 1
                if known >= 2:
                    turn_output(n - 2, entry, r % BANKS)
                    entry, r = entry + 1, r + 1
                scores(n, buf, 1)
                if maxima:
                    turn_maxima(n + 1, entry, r % BANKS)
                if known >= 1:
                    values(n - 1, (buf - 1) % BUFS, 1)

            for qb in range(QB):
                max_product(0, 0, qb, qb, qb % BANKS)
            turn_maxima(0, QB, QB % BANKS)
            step(0, 0, 0)
            step(1, 0, 1)
            in_groups(pe, 4, 2, HEADS - 2, step)
            step(HEADS - 2, (HEADS - 2) // 4, (HEADS - 2) % 4)
            n = HEADS - 1
            step(n, n // 4, n % 4, maxima=False)
            for t in range(NG):
                values(n, n % 4, t)
            entry = ring_base(n) + 1
            turn_output(n - 1, entry, entry % BANKS)
            turn_output(n, entry + 1, (entry + 1) % BANKS)

        @block.scalar
        def _(act):
            def step(n, turn, par):
                for t in range(NG):
                    scores = g["ps"][:, 2 * t:2 * t + 2, :].rearrange("p a c -> p (a c)")
                    act.wait_ge(s["scored"], n * NG + (t + 1))
                    if past(n):
                        act.wait_ge(s["low_pool" if t else "low_dve"], n)
                    nc.scalar.activation(m["full"][:, t, :], scores, ACT.Exp, scale=SCALE)
                    if past(n - 1):
                        act.wait_ge(s["pv"], (n - 1) * NG)
                    nc.scalar.activation(m["hi"][:, par * NG + t, :], scores, ACT.Exp, scale=SCALE).then_inc(s["p"], 1)

            step(0, 0, 0)
            step(1, 0, 1)
            in_pairs(act, 2, HEADS, step)

        @block.vector
        def _(dve):
            def read_max(qb, entry, slot):
                dve.wait_ge(s["ring_in"], entry + 1)
                nc.vector.tensor_reduce(m["mx"][:, qb:qb + 1], g["ps"][:, R + slot, :], AX_X, ALU.max).then_inc(s["ring_out"], 1)

            def finish_maxima(entry):
                dve.wait_ge(s["ring_out"], entry)
                nc.vector.tensor_scalar(m["row"][:], m["mx"][:], -1.0, None, ALU.mult).then_inc(s["maxed"], 1)

            def read_row(n, buf, entry, slot):
                dve.wait_ge(s["ring_in"], entry + 1)
                nc.vector.tensor_copy(m["q2"][SD:SD + 1, buf, :], g["ps"][SD:SD + 1, R + slot, :]).then_inc(s["row"], 1)
                dve.wait_ge(s["row"], n + 1)
                dve.sem_inc(s["ring_out"], 1)

            def low_part(n, par):
                dve.wait_ge(s["p"], n * NG + 1)
                nc.vector.tensor_tensor(m["lo"][:, par * NG, :], m["full"][:, 0, :],
                                        m["hi"][:, par * NG, :].bitcast(F32), ALU.subtract).then_inc(s["low_dve"], 1)

            def read_output(n):
                dve.wait_ge(s["pv"], (n + 1) * NG)
                nc.vector.tensor_copy(m["o"][0:VW, :], g["ps"][0:VW, O, :]).then_inc(s["out_read"], 1)

            def write_output(n, entry, slot):
                dve.wait_ge(s["ring_in"], entry + 1)
                turned = g["ps"][:, R + slot, :].rearrange("p (q c) -> p q c", q=QB)
                nc.vector.reciprocal(m["den"][:], turned[:, :, SD]).then_inc(s["inv"], 1)
                dve.wait_ge(s["inv"], n + 1)
                nc.vector.tensor_tensor(out.rearrange("p (b q) h d -> p b h q d", b=NB)[:, n // SH, n % SH],
                                        turned[:, :, 0:SD], m["den"][:].unsqueeze(2).to_broadcast([P, QB, SD]),
                                        ALU.mult).then_inc(s["ring_out"], 1)

            def step(n, turn, buf, maxima=True):
                entry, r = ring_base(n), ring_slots(n)
                known = n if isinstance(n, int) else 2
                if known >= 2:
                    read_output(n - 2)
                if maxima:
                    for qb in range(QB):
                        read_max(qb, entry, r % BANKS)
                        entry, r = entry + 1, r + 1
                    finish_maxima(entry)
                if known >= 2:
                    write_output(n - 2, entry, r % BANKS)
                    entry, r = entry + 1, r + 1
                if maxima:
                    read_row(n + 1, (buf + 1) % BUFS, entry, r % BANKS)
                low_part(n, buf % 2)

            dve.sem_inc(s["out_read"], 1)
            nc.vector.memset(words(m["k2"][SD:SD + 1]), 1.0).then_inc(s["ones"], 1)
            dve.wait_ge(s["ones"], 1)
            for qb in range(QB):
                read_max(qb, qb, qb % BANKS)
            finish_maxima(QB)
            read_row(0, 0, QB, QB % BANKS)
            step(0, 0, 0)
            step(1, 0, 1)
            in_groups(dve, 4, 2, HEADS - 2, step)
            step(HEADS - 2, (HEADS - 2) // 4, (HEADS - 2) % 4)
            n = HEADS - 1
            step(n, n // 4, n % 4, maxima=False)
            entry = ring_base(n) + 1
            read_output(n - 1)
            write_output(n - 1, entry, entry % BANKS)
            read_output(n)
            write_output(n, entry + 1, (entry + 1) % BANKS)


def dispatch(nc, g, xT, ins, sel, idx_col, gate, rows, rows_hi, rows_lo, xin_hi, xin_lo, early):
    PAIRS = NB * E
    TOP = 8
    NEG = -3.0e38
    OUTS = NB * KT * 2

    def chosen(part, n):
        b, k, half = n // (KT * 2), n // 2 % KT, n % 2
        return part[:, k, half * (E // 2):(half + 1) * (E // 2), b, :]

    def product(n):
        return g["ps"][:, n % 8, :].rearrange("p (e c) -> p e c", c=CAP)

    with ExitStack() as ctx:
        s = semaphores(nc, ctx, "rt", "landed early row_hi row_lo logits prob exped turned aff top turned2 spread done sel prod xhi read")
        m = buffers(nc, ctx, "rt", gw=([P, KT, E], F32), tok_col=([P, QB], F32),
                    mx=([P, ROWS], F32), p=([P, ROWS, E], F32), sum=([P, ROWS], F32), aff=([PAIRS, 2, S], F32),
                    val=([PAIRS, CAP], F32), idx=([PAIRS, CAP], U32), idxf=([PAIRS, CAP], F32))
        block = ctx.enter_context(nc.Block())

        @block.sync
        def _(sp):
            for dst, src in ((m["gw"], ins["gate_w"]), (m["tok_col"], ins["tok_col"])):
                sp.dma_start(dst[:], src).then_inc(s["landed"], 16)
            sp.wait_ge(s["early"], fetch(sp, s["early"], early))

        @block.gpsimd
        def _(pool):
            pool.wait_ge(s["logits"], 1)
            for t in range(ROWS):
                pool.wait_ge(s["row_hi"], t + 1)
                nc.gpsimd.tensor_tensor(rows_lo[:, t], rows[:, t], rows_hi[:, t].bitcast(F32), ALU.subtract).then_inc(s["row_lo"], 1)

        @block.tensor
        def _(pe):
            pe.wait_ge(s["landed"], 32)
            for t in range(ROWS):
                at = (t % QB * NB + t // QB) * E
                for k in range(KT):
                    last = nc.tensor.matmul(g["ps"][:, 0, at:at + E], xT[:, k, t * P:(t + 1) * P], m["gw"][:, k, :],
                                            start=(k == 0), stop=(k == KT - 1))
            last.then_inc(s["logits"], 1)
            pe.wait_ge(s["aff"], 1)
            for q in range(QB):
                last = nc.tensor.transpose(g["ps"][0:PAIRS, 1, q * P:(q + 1) * P], m["p"][:, q * NB:(q + 1) * NB, :].rearrange("p b e -> p (b e)"), g["ident"][:])
            last.then_inc(s["turned"], 1)
            pe.wait_ge(s["done"], 1)
            nc.tensor.transpose(g["ps"][:, 2, 0:PAIRS], m["val"][:], g["ident"][0:PAIRS, 0:PAIRS])
            nc.tensor.transpose(g["ps"][:, 2, PAIRS:2 * PAIRS], m["idxf"][:], g["ident"][0:PAIRS, 0:PAIRS]).then_inc(s["turned2"], 1)
            for r in range(PAIRS):
                last = nc.tensor.matmul(g["ps"][:, 4 + r // 4, r % 4 * P:(r % 4 + 1) * P],
                                        g["ident"][0:PAIRS, r:r + 1].to_broadcast([PAIRS, P]), m["idxf"][:], start=True, stop=True)
                if r % E == E - 1:
                    last.then_inc(s["spread"], 1)
            for n in range(OUTS):
                b, k, half = n // (KT * 2), n // 2 % KT, n % 2
                if n >= 8:
                    pe.wait_ge(s["read"], n - 7)
                elif n >= 2:
                    pe.wait_ge(s["sel"], 2 + QB * (2 if n >= 6 else 1))
                if n == 0:
                    pe.wait_ge(s["row_lo"], ROWS)
                count = 0
                for q in range(QB):
                    if n in (0, OUTS // NB):
                        pe.wait_ge(s["sel"], 2 + b * QB + q + 1)
                    for part in (rows_hi, rows_lo):
                        last = nc.tensor.matmul(g["ps"][:, n % 8, :], part[:, b * QB + q, k * P:(k + 1) * P],
                                                sel[:, b, q, half * BANK:(half + 1) * BANK],
                                                start=(count == 0), stop=(count == 2 * QB - 1))
                        count += 1
                last.then_inc(s["prod"], 1)

        @block.scalar
        def _(act):
            act.wait_ge(s["prob"], 2)
            nc.scalar.activation(m["p"][:], m["p"][:], ACT.Exp).then_inc(s["exped"], 1)
            for t in range(ROWS):
                nc.scalar.copy(rows_hi[:, t], rows[:, t]).then_inc(s["row_hi"], 1)
            for n in range(OUTS):
                act.wait_ge(s["prod"], n + 1)
                nc.scalar.copy(chosen(xin_hi, n), product(n)).then_inc(s["xhi"], 1)

        @block.vector
        def _(dve):
            dve.wait_ge(s["logits"], 1)
            logits = g["ps"][:, 0, 0:ROWS * E].rearrange("p (t e) -> p t e", e=E)
            nc.vector.tensor_reduce(m["mx"][:], logits, AX_X, ALU.max).then_inc(s["prob"], 1)
            dve.wait_ge(s["prob"], 1)
            nc.vector.tensor_tensor(m["p"][:], logits, m["mx"][:].unsqueeze(2).to_broadcast([P, ROWS, E]),
                                    ALU.subtract).then_inc(s["prob"], 1)
            dve.wait_ge(s["exped"], 1)
            nc.vector.tensor_reduce(m["sum"][:], m["p"][:], AX_X, ALU.add).then_inc(s["prob"], 1)
            dve.wait_ge(s["prob"], 3)
            nc.vector.reciprocal(m["mx"][:], m["sum"][:]).then_inc(s["prob"], 1)
            dve.wait_ge(s["prob"], 4)
            nc.vector.tensor_tensor(m["p"][:], m["p"][:], m["mx"][:].unsqueeze(2).to_broadcast([P, ROWS, E]), ALU.mult).then_inc(s["aff"], 1)
            dve.wait_ge(s["turned"], 1)
            nc.vector.tensor_copy(m["aff"][:, 0, :], g["ps"][0:PAIRS, 1, :]).then_inc(s["top"], 1)
            for r in range(CAP // TOP):
                best = m["val"][:, r * TOP:(r + 1) * TOP]
                dve.wait_ge(s["top"], max(3 * r, 1))
                nc.vector.max(best, m["aff"][:, r % 2, :]).then_inc(s["top"], 1)
                dve.wait_ge(s["top"], 3 * r + 2)
                nc.vector.match_replace(m["aff"][:, 1 - r % 2, :], best, m["aff"][:, r % 2, :], NEG).then_inc(s["top"], 1)
                nc.vector.max_index(m["idx"][:, r * TOP:(r + 1) * TOP], best, m["aff"][:, r % 2, :]).then_inc(s["top"], 1)
            dve.wait_ge(s["top"], 3 * (CAP // TOP) + 1)
            nc.vector.tensor_copy(m["idxf"][:], m["idx"][:]).then_inc(s["done"], 1)
            dve.wait_ge(s["turned2"], 1)
            nc.vector.tensor_copy(gate[:], g["ps"][:, 2, 0:PAIRS]).then_inc(s["sel"], 1)
            nc.vector.tensor_copy(idx_col[:], g["ps"][:, 2, PAIRS:2 * PAIRS]).then_inc(s["sel"], 1)
            for b in range(NB):
                dve.wait_ge(s["spread"], b + 1)
                spread = g["ps"][:, 4 + 2 * b:6 + 2 * b, :].rearrange("p a c -> p (a c)")
                for q in range(QB):
                    nc.vector.tensor_scalar(sel[:, b, q, :], spread, m["tok_col"][:, q:q + 1], None, ALU.is_equal).then_inc(s["sel"], 1)
            for n in range(OUTS):
                dve.wait_ge(s["xhi"], n + 1)
                nc.vector.tensor_tensor(chosen(xin_lo, n), product(n), chosen(xin_hi, n).bitcast(F32),
                                        ALU.subtract).then_inc(s["read"], 1)


def experts(nc, g, ins, xin_hi, xin_lo, gate, y, first_part):
    PART = 2 * P
    PARTS = INNER // PART
    IT = PART // P
    TOK = NB * CAP
    TILES = PARTS * IT
    LAG = 1
    HRING = 4
    GU = 2 * KT * PART
    WD = IT * D
    with ExitStack() as ctx:
        s = semaphores(nc, ctx, "ex", "w0 w1 guhi gulo dhi dlo hidden silu full hi lo down gcol y")
        w_in = (s["w0"], s["w1"])
        m = buffers(nc, ctx, "ex", w=([P, 2, GU + WD], F32), gu_hi=([P, 2, GU], F32R), gu_lo=([P, 2, GU], F32R),
                    d_hi=([P, 2, WD], F32R), d_lo=([P, 2, WD], F32R), silu=([P, 2, TOK], F32), full=([P, 2, TOK], F32),
                    hi=([P, HRING, TOK], F32R), lo=([P, HRING, TOK], F32R), gcol=([P, NB], F32))

        def landed(e, c):
            return first_part if isinstance(e, int) and e == 0 and c == 0 else m["w"][:, c % 2]

        Y = 4
        block = ctx.enter_context(nc.Block())

        @block.sync
        def _(sp):
            def step(e, first=False, last=False):
                for c in range(PARTS):
                    if not (first and c == 0 or last and c >= PARTS - 2):
                        sp.wait_ge(s["dlo"], e * PARTS + (c + 1))
                        sp.dma_start(m["w"][:, c % 2], ins["w_experts"][e + (c + 2) // PARTS, (c + 2) % PARTS]
                                     ).then_inc(w_in[c % 2], 16)

            sp.dma_start(m["w"][:, 1], ins["w_experts"][0, 1]).then_inc(w_in[1], 16)
            sp.dma_start(m["w"][:, 0], ins["w_experts"][0, 2]).then_inc(w_in[0], 16)
            step(0, first=True)
            with sp.Fori(1, E - 1) as e:
                step(e)
            step(E - 1, last=True)

        @block.tensor
        def _(pe):
            def hidden(e, t):
                c, i, n = t // IT, t % IT, e * TILES + t
                if i == 0:
                    pe.wait_ge(s["gulo"], e * PARTS + (c + 1))
                if past(n - 3):
                    pe.wait_ge(s["full"], n - 3)
                for w in range(2):
                    count = 0
                    for wp, xp in ((m["gu_hi"], xin_hi), (m["gu_hi"], xin_lo), (m["gu_lo"], xin_hi)):
                        for k in range(KT):
                            at = (w * KT + k) * PART + i * P
                            last = nc.tensor.matmul(g["ps"][:, t % 4, w * TOK:(w + 1) * TOK], wp[:, c % 2, at:at + P],
                                                    xp[:, k, e].rearrange("p b c -> p (b c)"),
                                                    start=(count == 0), stop=(count == 3 * KT - 1))
                            count += 1
                last.then_inc(s["hidden"], 1)

            def down(e, t, n):
                c, i = t // IT, t % IT
                pe.wait_ge(s["dlo"], e * PARTS + (c + 1))
                pe.wait_ge(s["lo"], n + 1)
                if t == 0 and past(n):
                    pe.wait_ge(s["y"], e * NB)
                for b in range(NB):
                    count = 0
                    for hp, wp in ((m["hi"], m["d_hi"]), (m["lo"], m["d_hi"]), (m["hi"], m["d_lo"])):
                        last = nc.tensor.matmul(g["ps"][:, Y + b, :], hp[:, t % HRING, b * CAP:(b + 1) * CAP],
                                                wp[:, c % 2, i * D:(i + 1) * D],
                                                start=(t == 0 and count == 0), stop=(t == TILES - 1 and count == 2))
                        count += 1
                last.then_inc(s["down"], 1)

            def step(e):
                first = isinstance(e, int) and e == 0
                for t in range(TILES):
                    hidden(e, t)
                    if t >= LAG:
                        down(e, t - LAG, e * TILES + (t - LAG))
                    elif not first:
                        down(e - 1, TILES - LAG + t, e * TILES + (t - LAG))

            step(0)
            with pe.Fori(1, E) as e:
                step(e)
            for t in range(TILES - LAG, TILES):
                down(E - 1, t, (E - 1) * TILES + t)

        @block.scalar
        def _(act):
            def split_gate_up(e, c):
                turns = e * (PARTS // 2) + (c // 2 + c % 2)
                if past(turns):
                    act.wait_ge(w_in[c % 2], turns * 16)
                if past(e * TILES + (c - 1) * IT):
                    act.wait_ge(s["hidden"], e * TILES + (c - 1) * IT)
                nc.scalar.copy(m["gu_hi"][:, c % 2], landed(e, c)[:, 0:GU]).then_inc(s["guhi"], 1)

            def split_down(e, c):
                if past(e * TILES + (c - 1) * IT):
                    act.wait_ge(s["down"], e * TILES + (c - 1) * IT)
                nc.scalar.copy(m["d_hi"][:, c % 2], landed(e, c)[:, GU:GU + WD]).then_inc(s["dhi"], 1)

            def step(e, last=False):
                for t in range(TILES):
                    n = e * TILES + t
                    act.wait_ge(s["hidden"], n + 1)
                    if past(n - 1):
                        act.wait_ge(s["full"], n - 1)
                    nc.scalar.activation(m["silu"][:, t % 2], g["ps"][:, t % 4, 0:TOK], ACT.Silu).then_inc(s["silu"], 1)
                    c = t // IT + 1
                    if last and c == PARTS:
                        continue
                    if t % IT == 0:
                        split_gate_up(e + c // PARTS, c % PARTS)
                    else:
                        split_down(e + c // PARTS, c % PARTS)

            split_gate_up(0, 0)
            split_down(0, 0)
            step(0)
            with act.Fori(1, E - 1) as e:
                step(e)
            step(E - 1, last=True)

        @block.vector
        def _(dve):
            def low_gate_up(e, c):
                dve.wait_ge(s["guhi"], e * PARTS + (c + 1))
                nc.vector.tensor_tensor(m["gu_lo"][:, c % 2], landed(e, c)[:, 0:GU], m["gu_hi"][:, c % 2].bitcast(F32),
                                        ALU.subtract).then_inc(s["gulo"], 1)

            def low_down(e, c):
                dve.wait_ge(s["dhi"], e * PARTS + (c + 1))
                nc.vector.tensor_tensor(m["d_lo"][:, c % 2], landed(e, c)[:, GU:GU + WD], m["d_hi"][:, c % 2].bitcast(F32),
                                        ALU.subtract).then_inc(s["dlo"], 1)

            def outputs(e):
                for b in range(NB):
                    nc.vector.tensor_copy(m["gcol"][:, b:b + 1], gate[:, b].unsqueeze(2)[:, e]).then_inc(s["gcol"], 1)
                dve.wait_ge(s["down"], (e + 1) * TILES)
                dve.wait_ge(s["gcol"], e * NB + NB)
                for b in range(NB):
                    nc.vector.tensor_scalar(y[:, b, e], g["ps"][:, Y + b, :], m["gcol"][:, b:b + 1], None,
                                            ALU.mult).then_inc(s["y"], 1)

            def step(e, last=False):
                first = isinstance(e, int) and e == 0
                for t in range(TILES):
                    n = e * TILES + t
                    dve.wait_ge(s["silu"], n + 1)
                    nc.vector.tensor_tensor(m["full"][:, t % 2], g["ps"][:, t % 4, TOK:2 * TOK], m["silu"][:, t % 2],
                                            ALU.mult).then_inc(s["full"], 1)
                    dve.wait_ge(s["full"], n + 1)
                    if past(n + 1 - HRING):
                        dve.wait_ge(s["down"], n + 1 - HRING)
                    nc.vector.tensor_copy(m["hi"][:, t % HRING], m["full"][:, t % 2]).then_inc(s["hi"], 1)
                    dve.wait_ge(s["hi"], n + 1)
                    nc.vector.tensor_tensor(m["lo"][:, t % HRING], m["full"][:, t % 2], m["hi"][:, t % HRING].bitcast(F32),
                                            ALU.subtract).then_inc(s["lo"], 1)
                    if t == 0 and not first:
                        outputs(e - 1)
                    c = t // IT + 1
                    if last and c == PARTS:
                        continue
                    if t % IT == 0:
                        low_gate_up(e + c // PARTS, c % PARTS)
                    else:
                        low_down(e + c // PARTS, c % PARTS)

            low_gate_up(0, 0)
            low_down(0, 0)
            step(0)
            with dve.Fori(1, E - 1) as e:
                step(e)
            step(E - 1, last=True)
            outputs(E - 1)


def scatter(nc, g, ins, idx_col, y, out):
    with ExitStack() as ctx:
        s = semaphores(nc, ctx, "sc", "landed onehot hi lo prod sum stored")
        m = buffers(nc, ctx, "sc", tok_row=([P, S], F32), at=([P, NB * E, S], F32R),
                    hi=([P, 4, D], F32R), lo=([P, 4, D], F32R))
        block = ctx.enter_context(nc.Block())

        @block.tensor
        def _(pe):
            for n in range(NB * E):
                b, e = n // E, n % E
                pe.wait_ge(s["onehot"], n + 1)
                pe.wait_ge(s["lo"], n + 1)
                for part in (m["hi"], m["lo"]):
                    for q in range(QB):
                        last = nc.tensor.matmul(g["ps"][:, b * QB + q, :], m["at"][:, n, q * P:(q + 1) * P], part[:, n % 4],
                                                start=(e == 0 and part is m["hi"]), stop=(e == E - 1 and part is m["lo"]))
                last.then_inc(s["prod"], 1)

        @block.scalar
        def _(act):
            for n in range(NB * E):
                if n >= 4:
                    act.wait_ge(s["prod"], n - 3)
                nc.scalar.copy(m["hi"][:, n % 4], y[:, n // E, n % E]).then_inc(s["hi"], 1)

        @block.vector
        def _(dve):
            def add(b):
                dve.wait_ge(s["prod"], (b + 1) * E)
                for t in range(b * QB, (b + 1) * QB):
                    nc.vector.tensor_tensor(g["x"][:, t, :], g["ps"][:, t, :], g["x"][:, t, :], ALU.add).then_inc(s["sum"], 1)

            dve.wait_ge(s["landed"], 16)
            for n in range(NB * E):
                nc.vector.tensor_scalar(m["at"][:, n, :], m["tok_row"][:], idx_col[:, n:n + 1], None,
                                        ALU.is_equal).then_inc(s["onehot"], 1)
                dve.wait_ge(s["hi"], n + 1)
                nc.vector.tensor_tensor(m["lo"][:, n % 4], y[:, n // E, n % E], m["hi"][:, n % 4].bitcast(F32),
                                        ALU.subtract).then_inc(s["lo"], 1)
                if n == E + 1:
                    add(0)
            add(1)

        @block.sync
        def _(sp):
            sp.dma_start(m["tok_row"][:], ins["tok_row"]).then_inc(s["landed"], 16)
            for t in range(ROWS):
                sp.wait_ge(s["sum"], t + 1)
                sp.dma_start(out[t * P:(t + 1) * P, :], g["x"][:, t, :]).then_inc(s["stored"], 16)
            sp.wait_ge(s["stored"], 16 * ROWS)


def perceiver_kernel(nc, ins, out):
    scr = {
        "q": nc.dram_tensor("scr_q", [2, NB * D, S], F32).ap(),
        "k": nc.dram_tensor("scr_k", [2, NB * CTX // BANK, D, BANK], F32).ap(),
        "v": nc.dram_tensor("scr_v", [NB * CTX // BANK, XH, P, (BANK // P) * (2 * XD + 1)], F32).ap(),
        "maskbias": nc.dram_tensor("scr_maskbias", [NB, CTX], F32).ap(),
        "ones": nc.dram_tensor("scr_ones", [1, CTX], F32).ap(),
        "sq": nc.dram_tensor("scr_sq", [2, NB, SH * SD, S], F32).ap(),
        "sk": nc.dram_tensor("scr_sk", [2, NB, SH * SD, S], F32).ap(),
    }
    with ExitStack() as whole:
        g = buffers(nc, whole, "all", x=([P, ROWS, D], F32), ident=([P, P], F32), fold=([P, XD + 1], F32),
                    stats=([P, ROWS, 6], F32), moments=([P, ROWS, 2], F32))
        g["ps"] = whole.enter_context(nc.psum_tensor("ps", [P, 8, BANK], F32))

        with ExitStack() as ctx:
            square = ([P, KT, D], F32)
            halves = ([P, KT, D], F32R)
            w = buffers(nc, ctx, "w0", wq=square, wk=square, wv=square, bq=([P, KT], F32), bk=([P, KT], F32),
                        wk_hi=halves, wk_lo=halves, wv_hi=halves, wv_lo=halves)
            c = buffers(nc, ctx, "c0", raw=([P, 2, KT, BANK], F32), mask=([P, 2, BANK], U8))
            with ExitStack() as latents:
                m = buffers(nc, latents, "x0", xT=([P, KT, NB * S], F32))
                normalise_rows(nc, g, "0", xT=m["xT"],
                               first=((g["x"][:], ins["x"].rearrange("(t p) d -> p t d", p=P)), (g["ident"][:], ins["ident"])),
                               early=((w["wq"][:], ins["xWq"]), (w["bq"][:], ins["xbq"]), (w["wk"][:], ins["xWk"]),
                                      (w["wv"][:], ins["xWv"]), (w["bk"][:], ins["xbk"]), (g["fold"][:], ins["fold"])))
                cross_queries(nc, g, m["xT"], ins, scr, w,
                              [(c["raw"][:, j], ins["ctx"][j]) for j in range(2)]
                              + [(c["mask"][:, j], ins["mask_tiles"][j].partition_broadcast(P)) for j in range(2)])
            project_context(nc, g, ins, scr, w, c)
        with ExitStack() as after:
            o = buffers(nc, after, "xo", o=([P, NB * XH, QB, XD], F32), w=([P, KT, D], F32), add=([P, D], F32), bias=([P, D], F32))
            g["o"] = o["o"]
            cross_attention(nc, g, ins, scr, ((o["w"][:], ins["xWo"]), (o["add"][:], ins["xbv"].partition_broadcast(P)),
                                              (o["bias"][:], ins["xbo"].partition_broadcast(P))))
            v = buffers(nc, after, "v", v=([P, ROWS, SH, SD + 1], F32))["v"]
            with ExitStack() as projecting:
                wide = ([P, 2, KT, SH * SD], F32R)
                w = buffers(nc, projecting, "sw", whole=([P, KT, SH * SD], F32), hi=wide, lo=wide)
                output_projection(nc, g, "x", lambda t: o["o"][:, t // QB * XH:(t // QB + 1) * XH, t % QB, :], D,
                                  o["w"], o["bias"], add=o["add"], split=(w["hi"][:, 0], w["lo"][:, 0], w["whole"]),
                                  load=ins["sWq"])
                xT = buffers(nc, projecting, "sx", hi=([P, KT, NB * S], F32R), lo=([P, KT, NB * S], F32R))
                normalise_rows(nc, g, "1", split=(xT["hi"], xT["lo"]))
                self_projections(nc, g, xT["hi"], xT["lo"], ins, scr, v[:], w["whole"], w["hi"], w["lo"])
            rows = buffers(nc, after, "so", o=([P, ROWS, SH, SD], F32))["o"]
            w_out = o["o"][:].rearrange("p n q d -> p (n q d)").rearrange("p (k d) -> p k d", d=D)
            self_attention(nc, g, ins, scr, v[:], rows[:], ((w_out, ins["sWo"]), (o["bias"][:], ins["sbo"].partition_broadcast(P))))
            output_projection(nc, g, "s", lambda t: rows[:, t].rearrange("p h d -> p (h d)"), SH * SD, w_out, o["bias"])
        with ExitStack() as ctx:
            m = buffers(nc, ctx, "m", idx_col=([P, NB * E], F32), gate=([P, NB * E], F32), y=([P, NB, E, D], F32))
            with ExitStack() as inner:
                xin = buffers(nc, inner, "xin", hi=([P, KT, E, NB, CAP], F32R), lo=([P, KT, E, NB, CAP], F32R))
                with ExitStack() as routing:
                    r = buffers(nc, routing, "r", rows=([P, ROWS, D], F32), hi=([P, ROWS, D], F32R),
                                sel=([P, NB, QB, E * CAP], F32R))
                    part = m["y"][:].rearrange("p b e d -> p (b e d)")[:, 0:ins["w_experts"].shape[3]]
                    with ExitStack() as turned:
                        xT = buffers(nc, turned, "t", xT=([P, KT, NB * S], F32))["xT"]
                        normalise_rows(nc, g, "2", xT, keep=r["rows"])
                    low = buffers(nc, routing, "low", rows=([P, ROWS, D], F32R))["rows"]
                    dispatch(nc, g, xT, ins, r["sel"], m["idx_col"], m["gate"], r["rows"], r["hi"], low,
                             xin["hi"], xin["lo"], ((part, ins["w_experts"][0, 0]),))
                experts(nc, g, ins, xin["hi"], xin["lo"], m["gate"][:].rearrange("p (b e) -> p b e", b=NB), m["y"], part)
            scatter(nc, g, ins, m["idx_col"], m["y"], out)


def laid_out(inputs):
    import numpy as np
    a = {n: np.asarray(v) for n, v in inputs.items()}

    def features(w):
        return w.reshape(-1, P, w.shape[1]).transpose(1, 0, 2)

    fold = np.zeros((P, XD + 1), np.float32)
    fold[:XD, :XD] = fold[XD:2 * XD, :XD] = np.eye(XD)
    fold[2 * XD, XD] = 1.0
    part = (E, INNER // (2 * P), 2 * P, KT, P)
    gate, up = (a[n].reshape(part).transpose(0, 1, 4, 3, 2).reshape(*part[:2], P, -1) for n in ("L0_ffn_w_gate", "L0_ffn_w_up"))
    down = a["L0_ffn_w_down"].reshape(E, D, part[1], 2, P).transpose(0, 2, 4, 3, 1).reshape(*part[:2], P, -1)
    experts = np.concatenate([gate, up, down], axis=3)
    said = {
        "x": a["x"].reshape(NB * S, D),
        "ctx": a["ctx_1024"].reshape(NB * CTX // BANK, BANK, KT, P).transpose(0, 3, 2, 1),
        "mask": a["mask_BxS2_bf1"].view(np.uint8).reshape(NB, CTX),
        "mask_tiles": a["mask_BxS2_bf1"].view(np.uint8).reshape(NB * CTX // BANK, BANK),
        "xWq": features(a["L0_xattn_Wq"].T), "xWk": features(a["L0_xattn_Wk"].T), "xWv": features(a["L0_xattn_Wv"].T),
        "xWo": features(a["L0_xattn_Wo"].T),
        "xbq": a["L0_xattn_bq"].reshape(KT, P).T, "xbk": a["L0_xattn_bk"].reshape(KT, P).T,
        "xbv": a["L0_xattn_bv"], "xbo": a["L0_xattn_bo"],
        "sWq": features(a["L0_attn_Wq"]), "sWk": features(a["L0_attn_Wk"]), "sWv": features(a["L0_attn_Wv"]),
        "sWo": features(a["L0_attn_Wo"]), "sbo": a["L0_attn_bo"],
        "gate_w": features(a["L0_ffn_gate_w"].T),
        "w_experts": experts,
        "ident": np.eye(P, dtype=np.float32), "fold": fold,
        "tok_row": np.broadcast_to(np.arange(S, dtype=np.float32), (P, S)),
        "tok_col": np.arange(S, dtype=np.float32).reshape(QB, P).T,
    }
    return {n: np.ascontiguousarray(v) for n, v in said.items()}


def kernel(**inputs):
    import numpy as np
    import concourse.bacc as bacc
    from concourse.bass_utils import run_bass_kernel_spmd

    nc = bacc.Bacc("TRN2", target_bir_lowering=False, num_devices=1)
    arrays, args = {}, {}
    for name, a in laid_out(inputs).items():
        arrays[f"in_{name}"] = a
        args[name] = nc.dram_tensor(f"in_{name}", a.shape, mybir.dt.from_np(a.dtype), kind="ExternalInput").ap()
    out = nc.dram_tensor("out", (NB * S, D), F32, kind="ExternalOutput").ap()
    perceiver_kernel(nc, args, out)
    r = run_bass_kernel_spmd(nc, [arrays], core_ids=[0])
    return r.results[0]["out"].reshape(NB, S, D)
```
